# Optimizing a Trainium2 kernel written in Bass

```python
import numpy as np
import jax
import jax.numpy as jnp

def _softmax(x, axis=-1):
    return jax.nn.softmax(x, axis=axis)

def _gelu(x):
    return jax.nn.gelu(x, approximate=True)

def _silu(x):
    return jax.nn.silu(x)

def _sigmoid(x):
    return jax.nn.sigmoid(x)

def _layernorm(x, axis=-1, eps=1e-05):
    m = jnp.mean(x, axis=axis, keepdims=True)
    v = jnp.var(x, axis=axis, keepdims=True)
    return (x - m) / jnp.sqrt(v + eps)

def _scatter_add(tgt, idx, src, axis=0):
    return tgt.at[idx].add(src)

def _segment_sum(src, seg, n):
    return jax.ops.segment_sum(src, seg, n)
kernel_name = 'mk_prb_d1_jaxref_r4_a7c8ca'

def setup_inputs(seed: int=0):
    np.random.seed(seed)
    _w = jnp.asarray

    def _L0_attn_setup():
        import jax, jax.numpy as jnp
        import numpy as np
        B, T, D_IN, D_PROJ, D_OUT, MEM = (8, 512, 256, 256, 256, 40)

        def _fsmn_memory(p, memory_weights):
            M = memory_weights.shape[0] - 1
            b, t, d = p.shape
            rhs = memory_weights[1:][::-1].T[:, None, :]
            lhs = jnp.pad(p.transpose(0, 2, 1), ((0, 0), (0, 0), (M - 1, 0)))
            band = jax.lax.conv_general_dilated(lhs, rhs, window_strides=(1,), padding='VALID', feature_group_count=d, dimension_numbers=('NCH', 'OIH', 'NCH')).transpose(0, 2, 1)
            cs = jnp.cumsum(p, axis=1)
            band_sum = cs - jnp.pad(cs, ((0, 0), (M, 0), (0, 0)))[:, :t]
            total = cs[:, -1:]
            return band + memory_weights[0] * (total - band_sum)
        key = jax.random.key(seed)
        k1, k2, k3, k4 = jax.random.split(key, 4)
        x = jax.random.normal(k1, (B, T, D_IN), dtype=jnp.float32)
        lim1 = np.sqrt(6.0 / (D_IN + D_PROJ))
        lim2 = np.sqrt(6.0 / (D_PROJ + D_OUT))
        limm = np.sqrt(6.0 / (MEM + 1 + D_PROJ))
        W1 = jax.random.uniform(k2, (D_IN, D_PROJ), minval=-lim1, maxval=lim1, dtype=jnp.float32)
        W2 = jax.random.uniform(k3, (D_PROJ, D_OUT), minval=-lim2, maxval=lim2, dtype=jnp.float32)
        mw = jax.random.uniform(k4, (MEM + 1, D_PROJ), minval=-limm, maxval=limm, dtype=jnp.float32)
        mw = mw.at[0].set(0.0)
        bias1 = jnp.ones((D_PROJ,), dtype=jnp.float32)
        bias2 = jnp.ones((D_OUT,), dtype=jnp.float32)
        return {'input_data': x, 'W1': W1, 'bias1': bias1, 'W2': W2, 'bias2': bias2, 'memory_weights': mw}
    _L0_attn_in = _L0_attn_setup()

    def _L0_ffn_setup():
        import jax, jax.numpy as jnp
        import numpy as np
        THRESH_FACTOR = 0.7

        def ternary_quantize(w):
            delta = THRESH_FACTOR * jnp.mean(jnp.abs(w))
            return jnp.where(w > delta, 1.0, jnp.where(w < -delta, -1.0, 0.0)).astype(w.dtype)
        key = jax.random.key(seed)
        k1, k2, k3 = jax.random.split(key, 3)
        B, S, D_IN, D_OUT = (8, 1024, 256, 256)
        inp = {'input': jax.random.normal(k1, (B, S, D_IN), dtype=jnp.float32), 'weight': jax.random.normal(k2, (D_OUT, D_IN), dtype=jnp.float32) * (1.0 / np.sqrt(D_IN)), 'alpha': jnp.ones((1,), dtype=jnp.float32), 'bias': jax.random.normal(k3, (D_OUT,), dtype=jnp.float32) * (1.0 / np.sqrt(D_IN))}
        return inp
    _L0_ffn_in = _L0_ffn_setup()
    _d = {'L0_attn_input_data': _L0_attn_in['input_data'], 'L0_attn_W1': _L0_attn_in['W1'], 'L0_attn_bias1': _L0_attn_in['bias1'], 'L0_attn_W2': _L0_attn_in['W2'], 'L0_attn_bias2': _L0_attn_in['bias2'], 'L0_attn_memory_weights': _L0_attn_in['memory_weights'], 'L0_ffn_weight': _L0_ffn_in['weight'], 'L0_ffn_alpha': _L0_ffn_in['alpha'], 'L0_ffn_bias': _L0_ffn_in['bias']}
    _x0 = _d['L0_attn_input_data']
    _d['L0_attn_input_data'] = jax.random.normal(jax.random.fold_in(jax.random.key(seed), 1), (2, 2048, 256), dtype=_x0.dtype)
    del _x0
    return _d

def reference(L0_attn_input_data, L0_attn_W1, L0_attn_bias1, L0_attn_W2, L0_attn_bias2, L0_attn_memory_weights, L0_ffn_weight, L0_ffn_alpha, L0_ffn_bias):

    def _L0_attn_ref(input_data, W1, bias1, W2, bias2, memory_weights):
        import jax, jax.numpy as jnp
        import numpy as np
        B, T, D_IN, D_PROJ, D_OUT, MEM = (8, 512, 256, 256, 256, 40)

        def _fsmn_memory(p, memory_weights):
            M = memory_weights.shape[0] - 1
            b, t, d = p.shape
            rhs = memory_weights[1:][::-1].T[:, None, :]
            lhs = jnp.pad(p.transpose(0, 2, 1), ((0, 0), (0, 0), (M - 1, 0)))
            band = jax.lax.conv_general_dilated(lhs, rhs, window_strides=(1,), padding='VALID', feature_group_count=d, dimension_numbers=('NCH', 'OIH', 'NCH')).transpose(0, 2, 1)
            cs = jnp.cumsum(p, axis=1)
            band_sum = cs - jnp.pad(cs, ((0, 0), (M, 0), (0, 0)))[:, :t]
            total = cs[:, -1:]
            return band + memory_weights[0] * (total - band_sum)
        p = jnp.matmul(input_data, W1) + bias1
        p = _fsmn_memory(p, memory_weights)
        return jnp.matmul(p, W2) + bias2

    def _L0_ffn_ref(input, weight, alpha, bias):
        import jax, jax.numpy as jnp
        import numpy as np
        THRESH_FACTOR = 0.7

        def ternary_quantize(w):
            delta = THRESH_FACTOR * jnp.mean(jnp.abs(w))
            return jnp.where(w > delta, 1.0, jnp.where(w < -delta, -1.0, 0.0)).astype(w.dtype)
        w_ternary = ternary_quantize(weight)
        w_eff = w_ternary * alpha
        out = jnp.einsum('bsd,od->bso', input, w_eff) + bias
        return out
    x = L0_attn_input_data
    xn = _layernorm(x, axis=-1)
    x = x + _L0_attn_ref(xn, L0_attn_W1, L0_attn_bias1, L0_attn_W2, L0_attn_bias2, L0_attn_memory_weights) + _L0_ffn_ref(xn, L0_ffn_weight, L0_ffn_alpha, L0_ffn_bias)
    return x

_drawn_inputs = setup_inputs


def setup_inputs(seed=0):
    import zlib

    import numpy as np

    out = dict(_drawn_inputs(seed))
    spreads = {'L0_attn_bias1': (1.0, 0.6), 'L0_attn_bias2': (1.0, 0.6)}
    factors = {'L0_ffn_bias': 8.0}
    for name, (base, spread) in spreads.items():
        noise = np.random.default_rng([zlib.crc32(name.encode()), seed]).standard_normal(out[name].shape)
        drawn = base * np.exp(spread * noise) if base else spread * noise
        out[name] = jnp.asarray(drawn.astype(out[name].dtype))
    for name, factor in factors.items():
        out[name] = (out[name] * factor).astype(out[name].dtype)
    return out
```

```python
import concourse.bass as bass
from concourse import mybir
from contextlib import ExitStack



def fsmn_ternary_layer(nc, x_in, W1_in, b1_in, W2_in, b2_in, mw_in, w_in, alpha_in, bias_in,
                       ident_in, tapsum_in, out):
    f32 = mybir.dt.float32
    f32r = mybir.dt.float32r
    ALU = mybir.AluOpType
    ACT = mybir.ActivationFunctionType
    AX = mybir.AxisListType

    B, S, D = x_in.shape
    TAPS = mw_in.shape[0] - 1
    P = 128
    KH = D // P
    TILES = B * S // P
    CH = 4
    N = CH * P
    CHUNKS = TILES // CH
    CPB = CHUNKS // B
    L = 32
    Q = P // L
    NB = S // L
    LAGS = (TAPS + L - 2) // L + 1
    LEAD = LAGS - 1
    G = KH * L
    GS = 4
    SLOTS = 4
    USES = G // GS // SLOTS
    RUN = LAGS * L
    WROW = P
    assert L - 1 + RUN <= WROW
    C_TAPS, C_TAIL, C_SUM, C_MW0, C_B1, C_ALL = 0, TAPS, 2 * TAPS, 2 * TAPS + 1, 2 * TAPS + 2, 2 * TAPS + 3
    EPS = 1e-5
    THRESH = 0.7 / (D * D)

    x_dram = x_in.rearrange("b (t p) c -> p (b t) c", p=P)
    out_dram = out.rearrange("b (t p) c -> p (b t) c", p=P)
    taps_dram = nc.dram_tensor("padded_taps", [Q, G, WROW], f32, kind="Internal")

    ctx = ExitStack()
    with ctx:
        def sb(name, shape, dt=f32):
            return ctx.enter_context(nc.sbuf_tensor(name, shape, dt))

        def sem(name):
            return ctx.enter_context(nc.semaphore(name))

        x = sb("x", [P, TILES, D])
        p = sb("p", [P, G, B, LEAD + NB])
        runs = sb("runs", [P, G, RUN])
        T = [sb(f"T{s}", [P, GS, LAGS, Q, L]) for s in range(SLOTS)]
        y = sb("y", [P, G, B * NB])
        yT0 = p[:, 0:L, :, :].rearrange("p g b n -> p (g b n)")[:, 0:B * S]
        yT1 = [sb(f"yT1_{j}", [P, N]) for j in range(2)]
        xn = [sb(f"xn{j}", [P, CH, D]) for j in range(2)]
        hi = [[sb(f"hi{j}{h}", [P, N], f32r) for h in range(KH)] for j in range(2)]
        lo = [[sb(f"lo{j}{h}", [P, N], f32r) for h in range(KH)] for j in range(2)]
        ffn = [sb(f"ffn{u}", [P, 2 * D]) for u in range(2)]
        stats = [sb(f"stats{j}", [P, CH, 6]) for j in range(2)]
        meanvar = [sb(f"meanvar{j}", [P, CH, 2]) for j in range(2)]
        var = [sb(f"var{j}", [P, CH]) for j in range(2)]
        std = [sb(f"std{j}", [P, CH]) for j in range(2)]
        rinv = [sb(f"rinv{j}", [P, CH]) for j in range(2)]
        newt = [sb(f"newt{j}", [P, CH]) for j in range(2)]
        newt2 = [sb(f"newt2{j}", [P, CH]) for j in range(2)]
        rstd = [sb(f"rstd{j}", [P, CH]) for j in range(2)]
        shift = [sb(f"shift{j}", [P, CH]) for j in range(2)]
        ident = sb("ident", [P, P])
        ones = sb("ones", [P, P])
        tapsum = sb("tapsum", [TAPS + 2, C_ALL])
        mw = sb("mw", [TAPS + 2, D])
        W1 = sb("W1", [P, KH, D])
        W2 = sb("W2", [P, KH, D])
        W1h, W1l = sb("W1h", [P, KH, D], f32r), sb("W1l", [P, KH, D], f32r)
        W2h, W2l = sb("W2h", [P, KH, D], f32r), sb("W2l", [P, KH, D], f32r)
        w = xn[1][:, 0:KH, :]
        tern = xn[1][:, KH:2 * KH, :]
        wneg = yT1[0][:, :].rearrange("p (h d) -> p h d", h=KH)
        wabs = sb("wabs", [P, 1])
        wT = sb("wT", [P, KH, D], f32r)
        delta = sb("delta", [P, 2])
        alpha = sb("alpha", [P, 1])
        biases = sb("biases", [P, 2, D])
        taps = sb("taps", [P, KH, C_ALL])
        wpad = sb("wpad", [P, KH, WROW])
        xsums = sb("xsums", [P, KH, CHUNKS])
        xsum = sb("xsum", [P, KH, B])
        total = sb("total", [P, KH, B])
        b1sum = sb("b1sum", [P, KH])
        const = sb("const", [P, KH, B])
        constT = sb("constT", [P, KH, B, P])
        tail = sb("tail", [P, KH, TAPS])
        biasrow = sb("biasrow", [P, D])
        rows = sb("rows", [P, B, D])
        edge = sb("edge", [TAPS, D])

        def bank(name):
            return ctx.enter_context(nc.psum_tensor(name, [P, N], f32))

        xT_ps = [bank(f"xT_ps{h}") for h in range(KH)]
        pT_ps = [bank(f"pT_ps{h}") for h in range(KH)]
        o_ps = [bank(f"o_ps{u}") for u in range(2)]
        y_ps = [bank(f"y_ps{u}") for u in range(2)]

        x_loaded = [sem(f"x_loaded{k}") for k in range(CHUNKS)]
        x_ready = sem("x_ready")
        W1_loaded, ident_loaded, mw_loaded = sem("W1_loaded"), sem("ident_loaded"), sem("mw_loaded")
        w_loaded, W2_loaded, small_loaded = sem("w_loaded"), sem("W2_loaded"), sem("small_loaded")
        zeroed = sem("zeroed")
        taps_mm, taps_done, wpad_done, taps_stored = sem("taps_mm"), sem("taps_done"), sem("wpad_done"), sem("taps_stored")
        wabs_done, wsum_mm, delta_done, ndelta_done = sem("wabs_done"), sem("wsum_mm"), sem("delta_done"), sem("ndelta_done")
        wneg_done, tern_done, wT_mm, wT_done = sem("wneg_done"), sem("tern_done"), sem("wT_mm"), sem("wT_done")
        W1h_done, W1l_done, W2h_done, W2l_done = sem("W1h_done"), sem("W1l_done"), sem("W2h_done"), sem("W2l_done")
        runs_loaded = sem("runs_loaded")
        T_built = [sem(f"T_built{s}") for s in range(SLOTS)]
        stats_done, agg_done, var_done, std_done = sem("stats_done"), sem("agg_done"), sem("var_done"), sem("std_done")
        rinv_done, newt_done, newt2_done, rstd_done = sem("rinv_done"), sem("newt_done"), sem("newt2_done"), sem("rstd_done")
        shift_done, xn_done = sem("shift_done"), sem("xn_done")
        xT_mm = [sem(f"xT_mm{h}") for h in range(KH)]
        hi_done = [sem(f"hi_done{h}") for h in range(KH)]
        lo_done = [sem(f"lo_done{h}") for h in range(KH)]
        pT_mm = [sem(f"pT_mm{h}") for h in range(KH)]
        p_done = [sem(f"p_done{h}") for h in range(KH)]
        o_mm = [sem(f"o_mm{u}") for u in range(2)]
        o_taken = [sem(f"o_taken{u}") for u in range(2)]
        ffn_added = [sem(f"ffn_added{u}") for u in range(2)]
        xsum_done, total_mm, const_a, const_done = sem("xsum_done"), sem("total_mm"), sem("const_a"), sem("const_done")
        constT_done, tail_done, rows_mm, edge_mm = sem("constT_done"), sem("tail_done"), sem("rows_mm"), sem("edge_mm")
        biasrow_done, rows_done, edge_done, rows_added, edge_added = (
            sem("biasrow_done"), sem("rows_done"), sem("edge_done"), sem("rows_added"), sem("edge_added"))
        y_mm = [sem(f"y_mm{u}") for u in range(2)]
        y_done = [sem(f"y_done{u}") for u in range(2)]
        yT0_done, yT1_done = sem("yT0_done"), sem("yT1_done")
        yhi_done = [sem(f"yhi_done{h}") for h in range(KH)]
        ylo_done = [sem(f"ylo_done{h}") for h in range(KH)]
        out_done = [sem(f"out_done{u}") for u in range(2)]
        out_stored = sem("out_stored")

        ds = bass.ds
        chunk_tiles = lambda k, first=0, count=CH: ds(k * CH + first, count)
        block = ctx.enter_context(nc.Block())

        def build_T(engine, s, q, use):
            rows_q = slice(q * L, (q + 1) * L)
            engine.tensor_copy(T[s][rows_q, :, :, q, :],
                               runs[rows_q, ds(use * (SLOTS * GS) + s * GS, GS), :].rearrange("p g (l j) -> p g l j", j=L)
                               ).then_inc(T_built[s], 1)

        @block.sync
        def _(sp):
            for k in range(CHUNKS):
                sp.dma_start(x[:, k * CH:(k + 1) * CH, :], x_dram[:, k * CH:(k + 1) * CH, :]).then_inc(x_loaded[k], 16)
                if k == 0:
                    sp.dma_start(W1[:, :, :], W1_in.rearrange("(h p) c -> p h c", p=P)).then_inc(W1_loaded, 16)
            for k in range(CHUNKS):
                sp.wait_ge(x_loaded[k], 16)
                sp.sem_inc(x_ready, 1)
            with sp.Fori(0, CHUNKS) as k:
                sp.wait_ge(out_done[0], k + 1)
                sp.wait_ge(out_done[1], k + 1)
                sp.dma_start(out_dram[:, chunk_tiles(k), :], x[:, chunk_tiles(k), :]).then_inc(out_stored, 16)
            sp.wait_ge(out_stored, 16 * CHUNKS)

        @block.gpsimd
        def _(pool):
            nc.gpsimd.memset(ones[:, :], 1.0).then_inc(zeroed, 1)
            nc.gpsimd.memset(wpad[:, :, :], 0.0).then_inc(zeroed, 1)
            for s in range(SLOTS):
                nc.gpsimd.memset(T[s][:, :, :, :, :], 0.0).then_inc(zeroed, 1)
            nc.gpsimd.memset(p[:, :, :, 0:LEAD], 0.0).then_inc(zeroed, 1)
            pool.wait_ge(small_loaded, 16 * 3)
            nc.gpsimd.tensor_tensor(biasrow[:, :], biases[:, 0, :], biases[:, 1, :], ALU.add).then_inc(biasrow_done, 1)
            builds = [(s, q) for s in range(SLOTS) for q in range(Q)]

            def first_builds(some):
                for s, q in some:
                    if q:
                        pool.wait_ge(T_built[s], q)
                    elif s:
                        pool.wait_ge(T_built[s - 1], Q)
                    build_T(nc.gpsimd, s, q, 0)
                if some:
                    s, q = some[-1]
                    pool.wait_ge(T_built[s], q + 1)

            for k in range(CHUNKS):
                if k == 1:
                    pool.wait_ge(runs_loaded, 16 * Q)
                    pool.wait_ge(zeroed, 3 + SLOTS)
                    pool.wait_ge(biasrow_done, 1)
                if k:
                    pool.wait_ge(ffn_added[1], k)
                    first_builds(builds[(k - 1) * 3:k * 3])
                for u in range(2):
                    pool.wait_ge(o_taken[u], k + 1)
                    at = x[:, chunk_tiles(k, 2 * u, 2), :]
                    nc.gpsimd.tensor_tensor(at, at, ffn[u][:, :].rearrange("p (t c) -> p t c", t=2),
                                            ALU.add).then_inc(ffn_added[u], 1)
            pool.wait_ge(ffn_added[1], CHUNKS)
            assert len(builds) <= 3 * (CHUNKS - 1)
            pool.wait_ge(rows_done, 1)
            for b in range(B):
                with pool.Fori(0, 2 * CPB) as k:
                    at = x[:, ds(k * 2 + b * (2 * 2 * CPB), 2), :]
                    pool.wait_ge(ffn_added[1], CHUNKS)
                    nc.gpsimd.tensor_tensor(at, at, rows[:, b:b + 1, :].to_broadcast([P, 2, D]),
                                            ALU.add).then_inc(rows_added, 1)
            pool.wait_ge(edge_done, 1)
            pool.wait_ge(rows_added, 2 * CHUNKS)
            for b in range(B):
                at = x[0:TAPS, b * CPB * CH, :]
                if b:
                    pool.wait_ge(edge_added, b)
                nc.gpsimd.tensor_tensor(at, at, edge[:, :], ALU.add).then_inc(edge_added, 1)
            pool.wait_ge(edge_added, B)
            def y_low(k, j):
                pool.wait_ge(yhi_done[0], k + 1)
                nc.gpsimd.tensor_tensor(lo[j][0][:, :], yT0[:, ds(k * N, N)], hi[j][0][:, :].bitcast(f32),
                                        ALU.subtract).then_inc(ylo_done[0], 1)

            with pool.Fori(0, CHUNKS // 2) as i:
                for j in range(2):
                    y_low(2 * i + j, j)

        @block.scalar
        def _(act):
            act.dma_start(ident[:, :], ident_in).then_inc(ident_loaded, 16)
            act.dma_start(mw[0:TAPS + 1, :], mw_in).then_inc(mw_loaded, 16)
            act.dma_start(mw[TAPS + 1:TAPS + 2, :], b1_in.rearrange("(a c) -> a c", a=1)).then_inc(mw_loaded, 16)
            act.dma_start(tapsum[:, :], tapsum_in).then_inc(mw_loaded, 16)
            act.dma_start(w, w_in.rearrange("(h p) d -> p h d", p=P)).then_inc(w_loaded, 16)
            act.dma_start(alpha[:, :], alpha_in.partition_broadcast(P)).then_inc(small_loaded, 16)
            act.dma_start(biases[:, 0, :], b2_in.partition_broadcast(P)).then_inc(small_loaded, 16)
            act.dma_start(biases[:, 1, :], bias_in.partition_broadcast(P)).then_inc(small_loaded, 16)
            act.dma_start(W2[:, :, :], W2_in.rearrange("(h p) c -> p h c", p=P)).then_inc(W2_loaded, 16)

            def root(k, j):
                act.wait_ge(var_done, k + 1)
                nc.scalar.activation(std[j][:, :], var[j][:, :], ACT.Sqrt).then_inc(std_done, 1)

            def normalise(k, j, reused):
                act.wait_ge(shift_done, k + 1)
                if reused:
                    act.wait_ge(xT_mm[KH - 1], k - 1)
                for t in range(CH):
                    last = nc.scalar.activation(xn[j][:, t, :], x[:, k * CH + t, :], ACT.Identity,
                                                bias=shift[j][:, t:t + 1], scale=rstd[j][:, t:t + 1])
                last.then_inc(xn_done, 1)

            def x_high(k, j, reused):
                for h in range(KH):
                    act.wait_ge(xT_mm[h], k + 1)
                    if reused and h == 0:
                        act.wait_ge(o_mm[1], k - 1)
                    nc.scalar.activation(hi[j][h][:, :], xT_ps[h][:, :], ACT.Copy,
                                         accum_out=xsums[:, h, ds(k, 1)]).then_inc(hi_done[h], 1)

            def take_ffn(k):
                for u in range(2):
                    act.wait_ge(o_mm[u], k + 1)
                    act.wait_ge(ffn_added[u], k)
                    nc.scalar.activation(ffn[u][:, :], o_ps[u][:, :], ACT.Copy,
                                         scale=alpha[:, 0:1]).then_inc(o_taken[u], 1)

            root(0, 0)
            act.wait_ge(W1_loaded, 16)
            nc.scalar.activation(W1h[:, :, :], W1[:, :, :], ACT.Copy).then_inc(W1h_done, 1)
            normalise(0, 0, False)
            act.wait_ge(w_loaded, 16)
            nc.scalar.activation(wneg, w, ACT.Abs, accum_out=wabs[:, 0:1]).then_inc(wabs_done, 1)
            root(1, 1)
            x_high(0, 0, False)
            act.wait_ge(W2_loaded, 16)
            nc.scalar.activation(W2h[:, :, :], W2[:, :, :], ACT.Copy).then_inc(W2h_done, 1)
            act.wait_ge(wT_mm, 1)
            nc.scalar.activation(wT[:, :, :], y_ps[1][:, :].rearrange("p (h o) -> p h o", h=KH),
                                 ACT.Copy).then_inc(wT_done, 1)
            act.wait_ge(wpad_done, 1)
            for q in range(Q):
                act.dma_start(taps_dram[q, :, :].rearrange("(h r) x -> r h x", h=KH),
                              wpad[q * L:(q + 1) * L, :, :]).then_inc(taps_stored, 16)
            act.wait_ge(taps_stored, 16 * Q)
            for q in range(Q):
                act.dma_start(runs[q * L:(q + 1) * L, :, :],
                              bass.AP(tensor=taps_dram, offset=q * G * WROW, ap=[[1, L], [WROW, G], [1, RUN]])
                              ).then_inc(runs_loaded, 16)
            act.wait_ge(small_loaded, 16 * 3)

            def first_phase(k, j, more=2):
                if more >= 1:
                    normalise(k + 1, 1 - j, True)
                if more >= 2:
                    root(k + 2, j)
                if more >= 1:
                    x_high(k + 1, 1 - j, True)
                take_ffn(k)

            for j in range(2):
                first_phase(j, j)
            with act.Fori(1, CHUNKS // 2 - 1) as i:
                for j in range(2):
                    first_phase(2 * i + j, j)
            first_phase(CHUNKS - 2, 0, more=1)
            first_phase(CHUNKS - 1, 1, more=0)

            def take_y(i, s):
                act.wait_ge(y_mm[s % 2], i * (SLOTS // 2) + s // 2 + 1)
                nc.scalar.activation(y[:, ds(i * (SLOTS * GS) + s * GS, GS), :],
                                     y_ps[s % 2][:, :].rearrange("p (g n) -> p g n", g=GS),
                                     ACT.Copy).then_inc(y_done[s % 2], 1)

            with act.Fori(0, USES) as i:
                for s in range(SLOTS):
                    take_y(i, s)

            def y_high(k, j):
                act.wait_ge(o_mm[1], k + CHUNKS - 1)
                act.wait_ge(yT0_done, k + 1)
                nc.scalar.activation(hi[j][0][:, :], yT0[:, ds(k * N, N)], ACT.Copy).then_inc(yhi_done[0], 1)
                act.wait_ge(yT1_done, k + 1)
                nc.scalar.activation(hi[j][1][:, :], yT1[j][:, :], ACT.Copy).then_inc(yhi_done[1], 1)

            with act.Fori(0, CHUNKS // 2) as i:
                for j in range(2):
                    y_high(2 * i + j, j)

        @block.vector
        def _(dve):
            V = nc.vector

            def statistics(k, j):
                dve.wait_ge(x_ready, k + 1)
                for t in range(CH):
                    last = V.bn_stats(stats[j][:, t, :], x[:, k * CH + t, :])
                last.then_inc(stats_done, 1)
                dve.wait_ge(stats_done, k + 1)
                for t in range(CH):
                    last = V.bn_aggr(meanvar[j][:, t, :], stats[j][:, t, :])
                last.then_inc(agg_done, 1)
                dve.wait_ge(agg_done, k + 1)
                V.tensor_scalar(var[j][:, :], meanvar[j][:, :, 1], EPS, None, ALU.add).then_inc(var_done, 1)

            def invert(k, j):
                dve.wait_ge(std_done, k + 1)
                V.reciprocal(rinv[j][:, :], std[j][:, :]).then_inc(rinv_done, 1)

            def newton_a(k, j):
                dve.wait_ge(rinv_done, k + 1)
                V.scalar_tensor_tensor(newt[j][:, :], rinv[j][:, :], -0.5, rinv[j][:, :],
                                       ALU.mult, ALU.mult).then_inc(newt_done, 1)

            def newton_b(k, j):
                dve.wait_ge(newt_done, k + 1)
                V.tensor_tensor(newt2[j][:, :], newt[j][:, :], var[j][:, :], ALU.mult).then_inc(newt2_done, 1)

            def newton_c(k, j):
                dve.wait_ge(newt2_done, k + 1)
                V.scalar_tensor_tensor(rstd[j][:, :], newt2[j][:, :], 1.5, rinv[j][:, :],
                                       ALU.add, ALU.mult).then_inc(rstd_done, 1)

            def shifts(k, j):
                dve.wait_ge(rstd_done, k + 1)
                V.scalar_tensor_tensor(shift[j][:, :], meanvar[j][:, :, 0], -1.0, rstd[j][:, :],
                                       ALU.mult, ALU.mult).then_inc(shift_done, 1)

            def x_low(k, j, h):
                dve.wait_ge(hi_done[h], k + 1)
                V.tensor_tensor(lo[j][h][:, :], xT_ps[h][:, :], hi[j][h][:, :].bitcast(f32),
                                ALU.subtract).then_inc(lo_done[h], 1)

            def to_filter_layout(k, h):
                dve.wait_ge(pT_mm[h], k + 1)
                dst = p[:, h * L:(h + 1) * L, ds(k // CPB, 1), ds((k % CPB) * (N // L) + LEAD, N // L)]
                V.transpose(dst.rearrange("p r b n -> p (b n) r"),
                            pT_ps[h][:, :].rearrange("p (n i) -> p n i", i=L)[:, :, ::-1]).then_inc(p_done[h], 1)

            statistics(0, 0)
            invert(0, 0)
            newton_a(0, 0)
            newton_b(0, 0)
            newton_c(0, 0)
            shifts(0, 0)
            statistics(1, 1)
            dve.wait_ge(W1h_done, 1)
            V.tensor_tensor(W1l[:, :, :], W1[:, :, :], W1h[:, :, :].bitcast(f32), ALU.subtract).then_inc(W1l_done, 1)
            dve.wait_ge(taps_mm, 1)
            V.tensor_copy(taps[:, :, :], y_ps[0][:, 0:KH * C_ALL].rearrange("p (h c) -> p h c", h=KH)).then_inc(taps_done, 1)
            dve.wait_ge(zeroed, 2)
            V.tensor_copy(wpad[:, :, L - 1:L - 1 + TAPS],
                          y_ps[0][:, 0:KH * C_ALL].rearrange("p (h c) -> p h c", h=KH)[:, :, 0:TAPS]).then_inc(wpad_done, 1)
            dve.wait_ge(wsum_mm, 1)
            V.tensor_scalar(delta[:, 0:1], y_ps[1][:, 0:1], THRESH, None, ALU.mult).then_inc(delta_done, 1)
            V.tensor_scalar(delta[:, 1:2], y_ps[1][:, 0:1], -THRESH, None, ALU.mult).then_inc(ndelta_done, 1)
            dve.wait_ge(ndelta_done, 1)
            V.tensor_scalar(wneg, w, delta[:, 1:2], None, ALU.is_lt).then_inc(wneg_done, 1)
            dve.wait_ge(wneg_done, 1)
            V.scalar_tensor_tensor(tern, w, delta[:, 0:1], wneg, ALU.is_gt, ALU.subtract).then_inc(tern_done, 1)
            x_low(0, 0, 0)
            x_low(0, 0, 1)
            invert(1, 1)
            newton_a(1, 1)
            newton_b(1, 1)
            newton_c(1, 1)
            shifts(1, 1)
            dve.wait_ge(W2h_done, 1)
            V.tensor_tensor(W2l[:, :, :], W2[:, :, :], W2h[:, :, :].bitcast(f32), ALU.subtract).then_inc(W2l_done, 1)

            def first_phase(k, j, more=2):
                if more >= 2:
                    statistics(k + 2, j)
                to_filter_layout(k, 0)
                if more >= 2:
                    invert(k + 2, j)
                to_filter_layout(k, 1)
                if more >= 2:
                    newton_a(k + 2, j)
                if more >= 1:
                    x_low(k + 1, 1 - j, 0)
                if more >= 2:
                    newton_b(k + 2, j)
                if more >= 1:
                    x_low(k + 1, 1 - j, 1)
                if more >= 2:
                    newton_c(k + 2, j)
                    shifts(k + 2, j)

            for k in range(CHUNKS - 2):
                first_phase(k, k % 2)
            first_phase(CHUNKS - 2, 0, more=1)

            V.tensor_reduce(xsum[:, :, :], xsums[:, :, :].rearrange("p h (b k) -> p h b k", b=B),
                            axis=AX.X, op=ALU.add).then_inc(xsum_done, 1)
            first_phase(CHUNKS - 1, 1, more=0)
            V.tensor_tensor(b1sum[:, :], taps[:, :, C_B1], taps[:, :, C_SUM], ALU.mult).then_inc(const_a, 1)
            for h in range(KH):
                last = V.tensor_scalar(tail[:, h, :], taps[:, h, C_TAIL:C_TAIL + TAPS], taps[:, h, C_B1:C_B1 + 1], None, ALU.mult)
            last.then_inc(tail_done, 1)
            dve.wait_ge(total_mm, 1)
            for h in range(KH):
                V.scalar_tensor_tensor(total[:, h, :], taps[:, h, C_B1:C_B1 + 1].to_broadcast([P, B]), float(S),
                                       xT_ps[0][:, B * h:B * h + B], ALU.mult, ALU.add).then_inc(const_a, 1)
            dve.wait_ge(const_a, 1 + KH)
            for h in range(KH):
                V.tensor_scalar(const[:, h, :], total[:, h, :], taps[:, h, C_MW0:C_MW0 + 1], b1sum[:, h:h + 1],
                                ALU.mult, ALU.add).then_inc(const_done, 1)
            dve.wait_ge(const_done, KH)
            V.tensor_copy(constT[:, :, :, :], const[:, :, :].unsqueeze(3).to_broadcast([P, KH, B, P])).then_inc(constT_done, 1)
            dve.wait_ge(rows_mm, 1)
            dve.wait_ge(biasrow_done, 1)
            for b in range(B):
                last = V.tensor_tensor(rows[:, b, :], xT_ps[1][:, b * D:(b + 1) * D], biasrow[:, :], ALU.add)
            last.then_inc(rows_done, 1)
            dve.wait_ge(edge_mm, 1)
            V.tensor_copy(edge[:, :], pT_ps[0][0:TAPS, 0:D]).then_inc(edge_done, 1)

            def from_filter_layout(dst, k, h):
                src = y[:, h * L:(h + 1) * L, ds(k * (N // L), N // L)].rearrange("p r n -> p n r")
                return V.transpose(dst.rearrange("p (n i) -> p n i", i=L), src)

            def rebuild_slot(i, s):
                dve.wait_ge(y_mm[s % 2], (i - 1) * (SLOTS // 2) + s // 2 + 1)
                for q in range(Q):
                    build_T(V, s, q, i)

            assert USES // KH + 1 == USES - 1
            with dve.Fori(1, USES - 1) as i:
                for s in range(SLOTS):
                    rebuild_slot(i, s)
            for u in range(2):
                dve.wait_ge(y_done[u], G // GS // KH // 2)
            for s in range(SLOTS):
                rebuild_slot(USES - 1, s)
                for k in range(s * CHUNKS // SLOTS, (s + 1) * CHUNKS // SLOTS):
                    from_filter_layout(yT0[:, ds(k * N, N)], k, 0).then_inc(yT0_done, 1)
            for u in range(2):
                dve.wait_ge(y_done[u], G // GS // 2)

            def y_second_half(k, j):
                from_filter_layout(yT1[j][:, :], k, 1).then_inc(yT1_done, 1)
                dve.wait_ge(yhi_done[1], k + 1)
                V.tensor_tensor(lo[j][1][:, :], yT1[j][:, :], hi[j][1][:, :].bitcast(f32),
                                ALU.subtract).then_inc(ylo_done[1], 1)

            def finish(k):
                for u in range(2):
                    dve.wait_ge(o_mm[u], k + CHUNKS + 1)
                    at = x[:, chunk_tiles(k, 2 * u, 2), :]
                    V.tensor_tensor(at, o_ps[u][:, :].rearrange("p (t c) -> p t c", t=2), at,
                                    ALU.add).then_inc(out_done[u], 1)

            y_second_half(0, 0)
            dve.wait_ge(rows_added, 2 * CHUNKS)
            dve.wait_ge(edge_added, B)
            for k in range(CHUNKS):
                if k + 1 < CHUNKS:
                    y_second_half(k + 1, (k + 1) % 2)
                finish(k)

        @block.tensor
        def _(pe):
            mm = nc.tensor.matmul

            def transposes(k, j):
                pe.wait_ge(xn_done, k + 1)
                for h in range(KH):
                    pe.wait_ge(lo_done[h], k)
                    for t in range(CH):
                        last = nc.tensor.transpose(xT_ps[h][:, t * P:(t + 1) * P], xn[j][:, t, h * P:(h + 1) * P], ident[:, :])
                    last.then_inc(xT_mm[h], 1)

            def project(k, j):
                for h in range(KH):
                    pe.wait_ge(p_done[h], k)
                    hs = slice(h * P, (h + 1) * P)
                    for d in range(KH):
                        if h == 0:
                            pe.wait_ge(hi_done[d], k + 1)
                        mm(pT_ps[h][:, :], W1h[:, d, hs], hi[j][d][:, :], start=(d == 0), stop=False)
                        mm(pT_ps[h][:, :], W1l[:, d, hs], hi[j][d][:, :], start=False, stop=False)
                    for d in range(KH):
                        if h == 0:
                            pe.wait_ge(lo_done[d], k + 1)
                        last = mm(pT_ps[h][:, :], W1h[:, d, hs], lo[j][d][:, :], start=False, stop=(d == KH - 1))
                    last.then_inc(pT_mm[h], 1)

            def feed_forward(k, j):
                for u in range(2):
                    pe.wait_ge(o_taken[u], k)
                    for t in range(2):
                        cols = slice((2 * u + t) * P, (2 * u + t + 1) * P)
                        for d in range(KH):
                            mm(o_ps[u][:, t * D:(t + 1) * D], hi[j][d][:, cols], wT[:, d, :], start=(d == 0), stop=False)
                            last = mm(o_ps[u][:, t * D:(t + 1) * D], lo[j][d][:, cols], wT[:, d, :],
                                      start=False, stop=(d == KH - 1))
                    last.then_inc(o_mm[u], 1)

            pe.wait_ge(mw_loaded, 16 * 3)
            for h in range(KH):
                last = mm(y_ps[0][:, h * C_ALL:(h + 1) * C_ALL], mw[:, h * P:(h + 1) * P], tapsum[:, :], start=True, stop=True)
            last.then_inc(taps_mm, 1)
            pe.wait_ge(ident_loaded, 16)
            transposes(0, 0)
            pe.wait_ge(zeroed, 1)
            pe.wait_ge(wabs_done, 1)
            mm(y_ps[1][:, 0:1], ones[:, :], wabs[:, :], start=True, stop=True).then_inc(wsum_mm, 1)
            pe.wait_ge(tern_done, 1)
            for d in range(KH):
                for o in range(KH):
                    last = nc.tensor.transpose(y_ps[1][:, d * D + o * P:d * D + (o + 1) * P], tern[:, o, d * P:(d + 1) * P], ident[:, :])
            last.then_inc(wT_mm, 1)
            pe.wait_ge(W1l_done, 1)
            pe.wait_ge(W1h_done, 1)

            def first_phase(k, j, more=True):
                project(k, j)
                if more:
                    transposes(k + 1, 1 - j)
                feed_forward(k, j)

            pe.wait_ge(wT_done, 1)
            for j in range(2):
                first_phase(j, j)
            with pe.Fori(1, CHUNKS // 2 - 1) as i:
                for j in range(2):
                    first_phase(2 * i + j, j)
            first_phase(CHUNKS - 2, 0)
            first_phase(CHUNKS - 1, 1, more=False)

            pe.wait_ge(xsum_done, 1)
            for h in range(KH):
                for d in range(KH):
                    last = mm(xT_ps[0][:, B * h:B * h + B], W1[:, d, h * P:(h + 1) * P], xsum[:, d, :],
                              start=(d == 0), stop=(d == KH - 1))
            last.then_inc(total_mm, 1)

            def filter_slot(i, s):
                pe.wait_ge(T_built[s], Q * (i + 1))
                pe.wait_ge(y_done[s % 2], i * (SLOTS // 2) + s // 2)
                for g in range(GS):
                    for lag in range(LAGS):
                        moving = p[:, ds(i * (SLOTS * GS) + s * GS + g, 1), :, LEAD - lag:LEAD - lag + NB]
                        last = mm(y_ps[s % 2][:, g * B * NB:(g + 1) * B * NB], T[s][:, g, lag, :, :].rearrange("p q j -> p (q j)"),
                                  moving.rearrange("p g b n -> p (g b) n"), start=(lag == 0), stop=(lag == LAGS - 1))
                last.then_inc(y_mm[s % 2], 1)

            for h in range(KH):
                pe.wait_ge(p_done[h], CHUNKS)
            pe.wait_ge(zeroed, 3 + SLOTS)
            filter_slot(0, 0)
            pe.wait_ge(constT_done, 1)
            pe.wait_ge(tail_done, 1)
            for b in range(B):
                for h in range(KH):
                    last = mm(xT_ps[1][:, b * D:(b + 1) * D], constT[:, h, b, :], W2[:, h, :], start=(h == 0), stop=(h == KH - 1))
            last.then_inc(rows_mm, 1)
            for h in range(KH):
                last = mm(pT_ps[0][0:TAPS, 0:D], tail[:, h, :], W2[:, h, :], start=(h == 0), stop=(h == KH - 1))
            last.then_inc(edge_mm, 1)
            for s in range(1, SLOTS):
                filter_slot(0, s)
            with pe.Fori(1, USES) as i:
                for s in range(SLOTS):
                    filter_slot(i, s)

            pe.wait_ge(W2l_done, 1)
            for u in range(2):
                pe.wait_ge(o_taken[u], CHUNKS)

            def output(k, j):
                for h in range(KH):
                    pe.wait_ge(yhi_done[h], k + 1)
                    pe.wait_ge(ylo_done[h], k + 1)
                for u in range(2):
                    pe.wait_ge(out_done[u], k)
                    for t in range(2):
                        cols = slice((2 * u + t) * P, (2 * u + t + 1) * P)
                        dst = o_ps[u][:, t * D:(t + 1) * D]
                        for h in range(KH):
                            mm(dst, hi[j][h][:, cols], W2h[:, h, :], start=(h == 0), stop=False)
                            mm(dst, hi[j][h][:, cols], W2l[:, h, :], start=False, stop=False)
                            last = mm(dst, lo[j][h][:, cols], W2h[:, h, :], start=False, stop=(h == KH - 1))
                    last.then_inc(o_mm[u], 1)

            for j in range(2):
                output(j, j)
            with pe.Fori(1, CHUNKS // 2) as i:
                for j in range(2):
                    output(2 * i + j, j)


_INS = ["L0_attn_input_data", "L0_attn_W1", "L0_attn_bias1", "L0_attn_W2", "L0_attn_bias2",
        "L0_attn_memory_weights", "L0_ffn_weight", "L0_ffn_alpha", "L0_ffn_bias"]


def _constants(taps):
    import numpy as np
    m = np.zeros((taps + 2, 2 * taps + 3), np.float32)
    for d in range(taps):
        m[1 + d, d] = 1
        m[0, d] = -1
        m[1 + d, taps:taps + d] = -1
        m[0, taps + d] = taps - 1 - d
    m[1:taps + 1, 2 * taps] = 1
    m[0, 2 * taps] = -taps
    m[0, 2 * taps + 1] = 1
    m[taps + 1, 2 * taps + 2] = 1
    return {"ident": np.eye(128, dtype=np.float32), "tapsum": m}


def kernel(**inputs):
    import numpy as np
    import concourse.bacc as bacc
    from concourse.bass_utils import run_bass_kernel_spmd

    nc = bacc.Bacc("TRN2", target_bir_lowering=False, num_devices=1)
    arrays, args = {}, []
    consts = _constants(inputs["L0_attn_memory_weights"].shape[0] - 1)
    for name, a in [(n, inputs[n]) for n in _INS] + list(consts.items()):
        a = np.ascontiguousarray(a)
        arrays[f"in_{name}_dram"] = a
        args.append(nc.dram_tensor(f"in_{name}_dram", a.shape, mybir.dt.from_np(a.dtype), kind="ExternalInput").ap())
    shape = inputs["L0_attn_input_data"].shape
    args.append(nc.dram_tensor("out_dram", shape, mybir.dt.float32, kind="ExternalOutput").ap())
    fsmn_ternary_layer(nc, *args)
    r = run_bass_kernel_spmd(nc, [arrays], core_ids=[0])
    return r.results[0]["out_dram"]
```

```python
import concourse.bass as bass
from concourse import mybir
from contextlib import ExitStack



def fsmn_ternary_layer(nc, x_in, W1_in, b1_in, W2_in, b2_in, mw_in, w_in, alpha_in, bias_in,
                       ident_in, tapsum_in, out):
    f32 = mybir.dt.float32
    f32r = mybir.dt.float32r
    ALU = mybir.AluOpType
    ACT = mybir.ActivationFunctionType
    AX = mybir.AxisListType

    B, S, D = x_in.shape
    TAPS = mw_in.shape[0] - 1
    P = 128
    KH = D // P
    TILES = B * S // P
    CH = 4
    N = CH * P
    CHUNKS = TILES // CH
    CPB = CHUNKS // B
    L = 32
    Q = P // L
    NB = S // L
    LAGS = (TAPS + L - 2) // L + 1
    LEAD = LAGS - 1
    G = KH * L
    GS = 4
    SLOTS = 4
    USES = G // GS // SLOTS
    RUN = LAGS * L
    WROW = P
    assert L - 1 + RUN <= WROW
    C_TAPS, C_TAIL, C_SUM, C_MW0, C_B1, C_ALL = 0, TAPS, 2 * TAPS, 2 * TAPS + 1, 2 * TAPS + 2, 2 * TAPS + 3
    EPS = 1e-5
    THRESH = 0.7 / (D * D)

    x_dram = x_in.rearrange("b (t p) c -> p (b t) c", p=P)
    out_dram = out.rearrange("b (t p) c -> p (b t) c", p=P)
    taps_dram = nc.dram_tensor("padded_taps", [Q, G, WROW], f32, kind="Internal")

    ctx = ExitStack()
    with ctx:
        def sb(name, shape, dt=f32):
            return ctx.enter_context(nc.sbuf_tensor(name, shape, dt))

        def sem(name):
            return ctx.enter_context(nc.semaphore(name))

        x = sb("x", [P, TILES, D])
        p = sb("p", [P, G, B, LEAD + NB])
        runs = sb("runs", [P, G, RUN])
        T = [sb(f"T{s}", [P, GS, LAGS, Q, L]) for s in range(SLOTS)]
        y = sb("y", [P, G, B * NB])
        yT0 = p[:, 0:L, :, :].rearrange("p g b n -> p (g b n)")[:, 0:B * S]
        yT1 = [sb(f"yT1_{j}", [P, N]) for j in range(2)]
        xn = [sb(f"xn{j}", [P, CH, D]) for j in range(2)]
        hi = [[sb(f"hi{j}{h}", [P, N], f32r) for h in range(KH)] for j in range(2)]
        lo = [[sb(f"lo{j}{h}", [P, N], f32r) for h in range(KH)] for j in range(2)]
        ffn = [sb(f"ffn{u}", [P, 2 * D]) for u in range(2)]
        stats = [sb(f"stats{j}", [P, CH, 6]) for j in range(2)]
        meanvar = [sb(f"meanvar{j}", [P, CH, 2]) for j in range(2)]
        var = [sb(f"var{j}", [P, CH]) for j in range(2)]
        std = [sb(f"std{j}", [P, CH]) for j in range(2)]
        rinv = [sb(f"rinv{j}", [P, CH]) for j in range(2)]
        newt = [sb(f"newt{j}", [P, CH]) for j in range(2)]
        newt2 = [sb(f"newt2{j}", [P, CH]) for j in range(2)]
        rstd = [sb(f"rstd{j}", [P, CH]) for j in range(2)]
        shift = [sb(f"shift{j}", [P, CH]) for j in range(2)]
        ident = sb("ident", [P, P])
        ones = sb("ones", [P, P])
        tapsum = sb("tapsum", [TAPS + 2, C_ALL])
        mw = sb("mw", [TAPS + 2, D])
        W1 = sb("W1", [P, KH, D])
        W2 = sb("W2", [P, KH, D])
        W1h, W1l = sb("W1h", [P, KH, D], f32r), sb("W1l", [P, KH, D], f32r)
        W2h, W2l = sb("W2h", [P, KH, D], f32r), sb("W2l", [P, KH, D], f32r)
        w, tern = (ffn[u][:, :].rearrange("p (h d) -> p h d", h=KH) for u in range(2))
        wneg = yT1[0][:, :].rearrange("p (h d) -> p h d", h=KH)
        wabs = sb("wabs", [P, 1])
        warm = sb("warm", [P, 1])
        wT = sb("wT", [P, KH, D], f32r)
        delta = sb("delta", [P, 2])
        alpha = sb("alpha", [P, 1])
        biases = sb("biases", [P, 2, D])
        taps = sb("taps", [P, KH, C_ALL])
        wpad = sb("wpad", [P, KH, WROW])
        xsums = sb("xsums", [P, KH, CHUNKS])
        xsum = sb("xsum", [P, KH, B])
        total = sb("total", [P, KH, B])
        b1sum = sb("b1sum", [P, KH])
        const = sb("const", [P, KH, B])
        constT = sb("constT", [P, KH, B, P])
        tail = sb("tail", [P, KH, TAPS])
        biasrow = sb("biasrow", [P, D])
        rows = sb("rows", [P, B, D])
        edge = sb("edge", [TAPS, D])

        def bank(name):
            return ctx.enter_context(nc.psum_tensor(name, [P, N], f32))

        xT_ps = [bank(f"xT_ps{h}") for h in range(KH)]
        pT_ps = [bank(f"pT_ps{h}") for h in range(KH)]
        o_ps = [bank(f"o_ps{u}") for u in range(2)]
        y_ps = [bank(f"y_ps{u}") for u in range(2)]
        out_ps = [o_ps, xT_ps]

        x_loaded = [sem(f"x_loaded{k}") for k in range(CHUNKS)]
        W1_loaded, ident_loaded, mw_loaded = sem("W1_loaded"), sem("ident_loaded"), sem("mw_loaded")
        w_loaded, W2_loaded, small_loaded = sem("w_loaded"), sem("W2_loaded"), sem("small_loaded")
        zeroed = sem("zeroed")
        taps_mm, taps_done, wpad_done, taps_stored = sem("taps_mm"), sem("taps_done"), sem("wpad_done"), sem("taps_stored")
        wabs_done, wsum_mm, delta_done, ndelta_done = sem("wabs_done"), sem("wsum_mm"), sem("delta_done"), sem("ndelta_done")
        wneg_done, tern_done, wT_mm, wT_done = sem("wneg_done"), sem("tern_done"), sem("wT_mm"), sem("wT_done")
        W1h_done, W1l_done, W2h_done, W2l_done = sem("W1h_done"), sem("W1l_done"), sem("W2h_done"), sem("W2l_done")
        runs_loaded = sem("runs_loaded")
        T_built = [sem(f"T_built{s}") for s in range(SLOTS)]
        stats_done, agg_done, var_done, std_done = sem("stats_done"), sem("agg_done"), sem("var_done"), sem("std_done")
        rinv_done, newt_done, newt2_done, rstd_done = sem("rinv_done"), sem("newt_done"), sem("newt2_done"), sem("rstd_done")
        shift_done, xn_done = sem("shift_done"), sem("xn_done")
        xT_mm = [sem(f"xT_mm{h}") for h in range(KH)]
        hi_done = [sem(f"hi_done{h}") for h in range(KH)]
        lo_done = [sem(f"lo_done{h}") for h in range(KH)]
        pT_mm = [sem(f"pT_mm{h}") for h in range(KH)]
        p_done = [sem(f"p_done{h}") for h in range(KH)]
        o_mm = [sem(f"o_mm{u}") for u in range(2)]
        o_taken = [sem(f"o_taken{u}") for u in range(2)]
        ffn_added = [sem(f"ffn_added{u}") for u in range(2)]
        xsum_done, total_mm, const_a, const_done = sem("xsum_done"), sem("total_mm"), sem("const_a"), sem("const_done")
        constT_done, tail_done, rows_mm, edge_mm = sem("constT_done"), sem("tail_done"), sem("rows_mm"), sem("edge_mm")
        biasrow_done, rows_done, edge_done, rows_added, edge_added = (
            sem("biasrow_done"), sem("rows_done"), sem("edge_done"), sem("rows_added"), sem("edge_added"))
        y_mm = [sem(f"y_mm{u}") for u in range(2)]
        y_done = [sem(f"y_done{u}") for u in range(2)]
        yT0_done, yT1_done = sem("yT0_done"), sem("yT1_done")
        yhi_done = [sem(f"yhi_done{h}") for h in range(KH)]
        ylo_done = [sem(f"ylo_done{h}") for h in range(KH)]
        out_done = [sem(f"out_done{u}") for u in range(2)]
        out_stored = sem("out_stored")

        ds = bass.ds
        chunk_tiles = lambda k, first=0, count=CH: ds(k * CH + first, count)
        block = ctx.enter_context(nc.Block())

        def build_T(engine, s, q, use):
            rows_q = slice(q * L, (q + 1) * L)
            engine.tensor_copy(T[s][rows_q, :, :, q, :],
                               runs[rows_q, ds(use * (SLOTS * GS) + s * GS, GS), :].rearrange("p g (l j) -> p g l j", j=L)
                               ).then_inc(T_built[s], 1)

        @block.sync
        def _(sp):
            def load_x(k):
                sp.dma_start(x[:, k * CH:(k + 1) * CH, :], x_dram[:, k * CH:(k + 1) * CH, :]).then_inc(x_loaded[k], 16)

            load_x(0)
            sp.dma_start(ident[:, :], ident_in).then_inc(ident_loaded, 16)
            sp.dma_start(W1[:, :, :], W1_in.rearrange("(h p) c -> p h c", p=P)).then_inc(W1_loaded, 16)
            load_x(1)
            sp.dma_start(w, w_in.rearrange("(h p) d -> p h d", p=P)).then_inc(w_loaded, 16)
            sp.dma_start(mw[0:TAPS + 1, :], mw_in).then_inc(mw_loaded, 16)
            sp.dma_start(mw[TAPS + 1:TAPS + 2, :], b1_in.rearrange("(a c) -> a c", a=1)).then_inc(mw_loaded, 16)
            sp.dma_start(tapsum[:, :], tapsum_in).then_inc(mw_loaded, 16)
            for k in range(2, CHUNKS // 2):
                load_x(k)
            sp.wait_ge(wpad_done, 1)
            for q in range(Q):
                sp.dma_start(taps_dram[q, :, :].rearrange("(h r) x -> r h x", h=KH),
                             wpad[q * L:(q + 1) * L, :, :]).then_inc(taps_stored, 16)
            for k in range(CHUNKS // 2, CHUNKS // 2 + 2):
                load_x(k)
            sp.wait_ge(taps_stored, 16 * Q)
            for q in range(Q):
                sp.dma_start(runs[q * L:(q + 1) * L, :, :],
                             bass.AP(tensor=taps_dram, offset=q * G * WROW, ap=[[1, L], [WROW, G], [1, RUN]])
                             ).then_inc(runs_loaded, 16)
            for k in range(CHUNKS // 2 + 2, CHUNKS):
                load_x(k)
            sp.dma_start(W2[:, :, :], W2_in.rearrange("(h p) c -> p h c", p=P)).then_inc(W2_loaded, 16)
            with sp.Fori(0, CHUNKS) as k:
                for u in range(2):
                    sp.wait_ge(out_done[u], k + 1)
                    sp.dma_start(out_dram[:, chunk_tiles(k, 2 * u, 2), :], x[:, chunk_tiles(k, 2 * u, 2), :]
                                 ).then_inc(out_stored, 16)
            sp.wait_ge(out_stored, 16 * 2 * CHUNKS)

        @block.gpsimd
        def _(pool):
            nc.gpsimd.memset(ones[:, :], 1.0).then_inc(zeroed, 1)
            nc.gpsimd.memset(wpad[:, :, :], 0.0).then_inc(zeroed, 1)
            for s in range(SLOTS):
                nc.gpsimd.memset(T[s][:, :, :, :, :], 0.0).then_inc(zeroed, 1)
            nc.gpsimd.memset(p[:, :, :, 0:LEAD], 0.0).then_inc(zeroed, 1)
            pool.dma_start(alpha[:, :], alpha_in.partition_broadcast(P)).then_inc(small_loaded, 16)
            pool.dma_start(biases[:, 0, :], b2_in.partition_broadcast(P)).then_inc(small_loaded, 16)
            pool.dma_start(biases[:, 1, :], bias_in.partition_broadcast(P)).then_inc(small_loaded, 16)
            pool.wait_ge(small_loaded, 16 * 3)
            nc.gpsimd.tensor_tensor(biasrow[:, :], biases[:, 0, :], biases[:, 1, :], ALU.add).then_inc(biasrow_done, 1)
            with pool.Fori(0, CHUNKS) as k:
                for u in range(2):
                    pool.wait_ge(o_taken[u], k + 1)
                    at = x[:, chunk_tiles(k, 2 * u, 2), :]
                    nc.gpsimd.tensor_tensor(at, at, ffn[u][:, :].rearrange("p (t c) -> p t c", t=2),
                                            ALU.add).then_inc(ffn_added[u], 1)
            pool.wait_ge(ffn_added[1], CHUNKS)
            pool.wait_ge(ffn_added[1], CHUNKS)
            pool.wait_ge(rows_done, 1)
            for b in range(B):
                with pool.Fori(0, 2 * CPB) as k:
                    at = x[:, ds(k * 2 + b * (2 * 2 * CPB), 2), :]
                    pool.wait_ge(ffn_added[1], CHUNKS)
                    nc.gpsimd.tensor_tensor(at, at, rows[:, b:b + 1, :].to_broadcast([P, 2, D]),
                                            ALU.add).then_inc(rows_added, 1)
            pool.wait_ge(edge_done, 1)
            pool.wait_ge(rows_added, 2 * CHUNKS)
            for b in range(B):
                at = x[0:TAPS, b * CPB * CH, :]
                if b:
                    pool.wait_ge(edge_added, b)
                nc.gpsimd.tensor_tensor(at, at, edge[:, :], ALU.add).then_inc(edge_added, 1)
            pool.wait_ge(edge_added, B)
            def y_low(k, j):
                pool.wait_ge(yhi_done[0], k + 1)
                nc.gpsimd.tensor_tensor(lo[j][0][:, :], yT0[:, ds(k * N, N)], hi[j][0][:, :].bitcast(f32),
                                        ALU.subtract).then_inc(ylo_done[0], 1)

            with pool.Fori(0, CHUNKS // 2) as i:
                for j in range(2):
                    y_low(2 * i + j, j)

        @block.scalar
        def _(act):
            def root(k, j):
                act.wait_ge(var_done, k + 1)
                nc.scalar.activation(std[j][:, :], var[j][:, :], ACT.Sqrt).then_inc(std_done, 1)

            def normalise(k, j, reused):
                act.wait_ge(shift_done, k + 1)
                if reused:
                    act.wait_ge(xT_mm[KH - 1], k - 1)
                for t in range(CH):
                    last = nc.scalar.activation(xn[j][:, t, :], x[:, k * CH + t, :], ACT.Identity,
                                                bias=shift[j][:, t:t + 1], scale=rstd[j][:, t:t + 1])
                last.then_inc(xn_done, 1)

            def x_high(k, j, reused):
                for h in range(KH):
                    act.wait_ge(xT_mm[h], k + 1)
                    if reused and h == 0:
                        act.wait_ge(o_mm[1], k - 1)
                    nc.scalar.activation(hi[j][h][:, :], xT_ps[h][:, :], ACT.Copy,
                                         accum_out=xsums[:, h, ds(k, 1)]).then_inc(hi_done[h], 1)

            def take_ffn(k):
                for u in range(2):
                    act.wait_ge(o_mm[u], k + 1)
                    act.wait_ge(ffn_added[u], k)
                    nc.scalar.activation(ffn[u][:, :], o_ps[u][:, :], ACT.Copy,
                                         scale=alpha[:, 0:1]).then_inc(o_taken[u], 1)

            act.wait_ge(zeroed, 1)
            nc.scalar.activation(warm[:, :], ones[:, 0:1], ACT.Sqrt)
            act.wait_ge(W1_loaded, 16)
            nc.scalar.activation(W1h[:, :, :], W1[:, :, :], ACT.Copy).then_inc(W1h_done, 1)
            root(0, 0)
            normalise(0, 0, False)
            root(1, 1)
            act.wait_ge(w_loaded, 16)
            nc.scalar.activation(wneg, w, ACT.Abs, accum_out=wabs[:, 0:1]).then_inc(wabs_done, 1)
            x_high(0, 0, False)
            normalise(1, 1, False)
            act.wait_ge(wT_mm, 1)
            nc.scalar.activation(wT[:, :, :], y_ps[1][:, :].rearrange("p (h o) -> p h o", h=KH),
                                 ACT.Copy).then_inc(wT_done, 1)
            act.wait_ge(small_loaded, 16 * 3)

            def first_phase(k, j, more=2):
                if more >= 2:
                    root(k + 2, j)
                if more >= 1:
                    x_high(k + 1, 1 - j, True)
                if more >= 2:
                    normalise(k + 2, j, True)
                take_ffn(k)

            for j in range(2):
                first_phase(j, j)
            with act.Fori(1, CHUNKS // 2 - 1) as i:
                for j in range(2):
                    first_phase(2 * i + j, j)
            first_phase(CHUNKS - 2, 0, more=1)
            first_phase(CHUNKS - 1, 1, more=0)
            act.wait_ge(W2_loaded, 16)
            nc.scalar.activation(W2h[:, :, :], W2[:, :, :], ACT.Copy).then_inc(W2h_done, 1)

            def take_y(i, s):
                act.wait_ge(y_mm[s % 2], i * (SLOTS // 2) + s // 2 + 1)
                nc.scalar.activation(y[:, ds(i * (SLOTS * GS) + s * GS, GS), :],
                                     y_ps[s % 2][:, :].rearrange("p (g n) -> p g n", g=GS),
                                     ACT.Copy).then_inc(y_done[s % 2], 1)

            def y_high_first(k, j):
                act.wait_ge(o_mm[1], k + CHUNKS - 1)
                act.wait_ge(yT0_done, k + 1)
                nc.scalar.activation(hi[j][0][:, :], yT0[:, ds(k * N, N)], ACT.Copy).then_inc(yhi_done[0], 1)

            def y_high_second(k, j):
                act.wait_ge(yT1_done, k + 1)
                nc.scalar.activation(hi[j][1][:, :], yT1[j][:, :], ACT.Copy).then_inc(yhi_done[1], 1)

            with act.Fori(0, USES - 1) as i:
                for s in range(SLOTS):
                    take_y(i, s)
            for s in range(SLOTS - 1):
                take_y(USES - 1, s)
            for j in range(2):
                y_high_first(j, j)
            take_y(USES - 1, SLOTS - 1)
            for j in range(2):
                y_high_second(j, j)
            with act.Fori(1, CHUNKS // 2) as i:
                for j in range(2):
                    y_high_first(2 * i + j, j)
                    y_high_second(2 * i + j, j)

        @block.vector
        def _(dve):
            V = nc.vector

            def statistics(k, j):
                dve.wait_ge(x_loaded[k], 16)
                for t in range(CH):
                    last = V.bn_stats(stats[j][:, t, :], x[:, k * CH + t, :])
                last.then_inc(stats_done, 1)
                dve.wait_ge(stats_done, k + 1)
                for t in range(CH):
                    last = V.bn_aggr(meanvar[j][:, t, :], stats[j][:, t, :])
                last.then_inc(agg_done, 1)
                dve.wait_ge(agg_done, k + 1)
                V.tensor_scalar(var[j][:, :], meanvar[j][:, :, 1], EPS, None, ALU.add).then_inc(var_done, 1)

            def invert(k, j):
                dve.wait_ge(std_done, k + 1)
                V.reciprocal(rinv[j][:, :], std[j][:, :]).then_inc(rinv_done, 1)

            def newton_a(k, j):
                dve.wait_ge(rinv_done, k + 1)
                V.scalar_tensor_tensor(newt[j][:, :], rinv[j][:, :], -0.5, rinv[j][:, :],
                                       ALU.mult, ALU.mult).then_inc(newt_done, 1)

            def newton_b(k, j):
                dve.wait_ge(newt_done, k + 1)
                V.tensor_tensor(newt2[j][:, :], newt[j][:, :], var[j][:, :], ALU.mult).then_inc(newt2_done, 1)

            def newton_c(k, j):
                dve.wait_ge(newt2_done, k + 1)
                V.scalar_tensor_tensor(rstd[j][:, :], newt2[j][:, :], 1.5, rinv[j][:, :],
                                       ALU.add, ALU.mult).then_inc(rstd_done, 1)

            def shifts(k, j):
                dve.wait_ge(rstd_done, k + 1)
                V.scalar_tensor_tensor(shift[j][:, :], meanvar[j][:, :, 0], -1.0, rstd[j][:, :],
                                       ALU.mult, ALU.mult).then_inc(shift_done, 1)

            def x_low(k, j, h):
                dve.wait_ge(hi_done[h], k + 1)
                V.tensor_tensor(lo[j][h][:, :], xT_ps[h][:, :], hi[j][h][:, :].bitcast(f32),
                                ALU.subtract).then_inc(lo_done[h], 1)

            def to_filter_layout(k, h):
                dve.wait_ge(pT_mm[h], k + 1)
                dst = p[:, h * L:(h + 1) * L, ds(k // CPB, 1), ds((k % CPB) * (N // L) + LEAD, N // L)]
                V.transpose(dst.rearrange("p r b n -> p (b n) r"),
                            pT_ps[h][:, :].rearrange("p (n i) -> p n i", i=L)[:, :, ::-1]).then_inc(p_done[h], 1)

            statistics(0, 0)
            invert(0, 0)
            newton_a(0, 0)
            newton_b(0, 0)
            newton_c(0, 0)
            shifts(0, 0)
            statistics(1, 1)
            dve.wait_ge(W1h_done, 1)
            V.tensor_tensor(W1l[:, :, :], W1[:, :, :], W1h[:, :, :].bitcast(f32), ALU.subtract).then_inc(W1l_done, 1)
            invert(1, 1)
            newton_a(1, 1)
            newton_b(1, 1)
            newton_c(1, 1)
            shifts(1, 1)
            x_low(0, 0, 0)
            x_low(0, 0, 1)
            dve.wait_ge(zeroed, 2)
            dve.wait_ge(taps_mm, 1)
            V.tensor_copy(wpad[:, :, L - 1:L - 1 + TAPS],
                          y_ps[0][:, 0:KH * C_ALL].rearrange("p (h c) -> p h c", h=KH)[:, :, 0:TAPS]).then_inc(wpad_done, 1)
            V.tensor_copy(taps[:, :, :], y_ps[0][:, 0:KH * C_ALL].rearrange("p (h c) -> p h c", h=KH)).then_inc(taps_done, 1)
            dve.wait_ge(wsum_mm, 1)
            V.tensor_scalar(delta[:, 0:1], y_ps[1][:, 0:1], THRESH, None, ALU.mult).then_inc(delta_done, 1)
            V.tensor_scalar(delta[:, 1:2], y_ps[1][:, 0:1], -THRESH, None, ALU.mult).then_inc(ndelta_done, 1)
            dve.wait_ge(ndelta_done, 1)
            V.tensor_scalar(wneg, w, delta[:, 1:2], None, ALU.is_lt).then_inc(wneg_done, 1)
            dve.wait_ge(wneg_done, 1)
            V.scalar_tensor_tensor(tern, w, delta[:, 0:1], wneg, ALU.is_gt, ALU.subtract).then_inc(tern_done, 1)

            def first_phase(k, j, more=2):
                if more >= 2:
                    statistics(k + 2, j)
                to_filter_layout(k, 0)
                if more >= 2:
                    invert(k + 2, j)
                to_filter_layout(k, 1)
                if more >= 2:
                    newton_a(k + 2, j)
                    newton_b(k + 2, j)
                    newton_c(k + 2, j)
                    shifts(k + 2, j)
                if more >= 1:
                    x_low(k + 1, 1 - j, 0)
                    x_low(k + 1, 1 - j, 1)

            for k in range(CHUNKS - 2):
                first_phase(k, k % 2)
            dve.wait_ge(runs_loaded, 16 * Q)
            dve.wait_ge(zeroed, 3 + SLOTS)

            def build_slot(s, i):
                for q in range(Q):
                    build_T(V, s, q, i)

            build_slot(0, 0)
            first_phase(CHUNKS - 2, 0, more=1)
            build_slot(1, 0)
            V.tensor_reduce(xsum[:, :, :], xsums[:, :, :].rearrange("p h (b k) -> p h b k", b=B),
                            axis=AX.X, op=ALU.add).then_inc(xsum_done, 1)
            first_phase(CHUNKS - 1, 1, more=0)
            V.tensor_tensor(b1sum[:, :], taps[:, :, C_B1], taps[:, :, C_SUM], ALU.mult).then_inc(const_a, 1)
            for h in range(KH):
                last = V.tensor_scalar(tail[:, h, :], taps[:, h, C_TAIL:C_TAIL + TAPS], taps[:, h, C_B1:C_B1 + 1], None, ALU.mult)
            last.then_inc(tail_done, 1)
            dve.wait_ge(total_mm, 1)
            for h in range(KH):
                V.scalar_tensor_tensor(total[:, h, :], taps[:, h, C_B1:C_B1 + 1].to_broadcast([P, B]), float(S),
                                       xT_ps[0][:, B * h:B * h + B], ALU.mult, ALU.add).then_inc(const_a, 1)
            dve.wait_ge(const_a, 1 + KH)
            for h in range(KH):
                V.tensor_scalar(const[:, h, :], total[:, h, :], taps[:, h, C_MW0:C_MW0 + 1], b1sum[:, h:h + 1],
                                ALU.mult, ALU.add).then_inc(const_done, 1)
            dve.wait_ge(const_done, KH)
            V.tensor_copy(constT[:, :, :, :], const[:, :, :].unsqueeze(3).to_broadcast([P, KH, B, P])).then_inc(constT_done, 1)
            dve.wait_ge(rows_mm, 1)
            dve.wait_ge(biasrow_done, 1)
            for b in range(B):
                last = V.tensor_tensor(rows[:, b, :], xT_ps[1][:, b * D:(b + 1) * D], biasrow[:, :], ALU.add)
            last.then_inc(rows_done, 1)
            dve.wait_ge(edge_mm, 1)
            V.tensor_copy(edge[:, :], pT_ps[0][0:TAPS, 0:D]).then_inc(edge_done, 1)

            def from_filter_layout(dst, k, h):
                src = y[:, h * L:(h + 1) * L, ds(k * (N // L), N // L)].rearrange("p r n -> p n r")
                return V.transpose(dst.rearrange("p (n i) -> p n i", i=L), src)

            for s in range(2, SLOTS):
                build_slot(s, 0)

            def rebuild_slot(i, s):
                dve.wait_ge(y_mm[s % 2], (i - 1) * (SLOTS // 2) + s // 2 + 1)
                build_slot(s, i)

            assert USES // KH + 1 == USES - 1
            with dve.Fori(1, USES - 1) as i:
                for s in range(SLOTS):
                    rebuild_slot(i, s)
            dve.wait_ge(W2h_done, 1)
            V.tensor_tensor(W2l[:, :, :], W2[:, :, :], W2h[:, :, :].bitcast(f32), ALU.subtract).then_inc(W2l_done, 1)
            for u in range(2):
                dve.wait_ge(y_done[u], G // GS // KH // 2)
            for s in range(SLOTS):
                rebuild_slot(USES - 1, s)
                for k in range(s * CHUNKS // SLOTS, (s + 1) * CHUNKS // SLOTS):
                    from_filter_layout(yT0[:, ds(k * N, N)], k, 0).then_inc(yT0_done, 1)
            for u in range(2):
                dve.wait_ge(y_done[u], G // GS // 2)

            def y_transposed(k, j):
                if k >= 2:
                    dve.wait_ge(ylo_done[1], k - 1)
                from_filter_layout(yT1[j][:, :], k, 1).then_inc(yT1_done, 1)

            def y_low(k, j):
                dve.wait_ge(yhi_done[1], k + 1)
                V.tensor_tensor(lo[j][1][:, :], yT1[j][:, :], hi[j][1][:, :].bitcast(f32),
                                ALU.subtract).then_inc(ylo_done[1], 1)

            def finish(k, u):
                dve.wait_ge(o_mm[u], k + CHUNKS + 1)
                at = x[:, chunk_tiles(k, 2 * u, 2), :]
                V.tensor_tensor(at, out_ps[k % 2][u][:, :].rearrange("p (t c) -> p t c", t=2), at,
                                ALU.add).then_inc(out_done[u], 1)

            for k in range(2):
                y_transposed(k, k)
                y_low(k, k)
            y_transposed(2, 0)
            dve.wait_ge(rows_added, 2 * CHUNKS)
            dve.wait_ge(edge_added, B)
            for k in range(CHUNKS):
                finish(k, 0)
                if k + 3 < CHUNKS:
                    y_transposed(k + 3, (k + 3) % 2)
                finish(k, 1)
                if k + 2 < CHUNKS:
                    y_low(k + 2, k % 2)

        @block.tensor
        def _(pe):
            mm = nc.tensor.matmul

            def transposes(k, j):
                pe.wait_ge(xn_done, k + 1)
                for h in range(KH):
                    pe.wait_ge(lo_done[h], k)
                    for t in range(CH):
                        last = nc.tensor.transpose(xT_ps[h][:, t * P:(t + 1) * P], xn[j][:, t, h * P:(h + 1) * P], ident[:, :])
                    last.then_inc(xT_mm[h], 1)

            def project(k, j):
                for h in range(KH):
                    pe.wait_ge(p_done[h], k)
                    hs = slice(h * P, (h + 1) * P)
                    for d in range(KH):
                        if h == 0:
                            pe.wait_ge(hi_done[d], k + 1)
                        mm(pT_ps[h][:, :], W1h[:, d, hs], hi[j][d][:, :], start=(d == 0), stop=False)
                        mm(pT_ps[h][:, :], W1l[:, d, hs], hi[j][d][:, :], start=False, stop=False)
                    for d in range(KH):
                        if h == 0:
                            pe.wait_ge(lo_done[d], k + 1)
                        last = mm(pT_ps[h][:, :], W1h[:, d, hs], lo[j][d][:, :], start=False, stop=(d == KH - 1))
                    last.then_inc(pT_mm[h], 1)

            def feed_forward(k, j):
                for u in range(2):
                    pe.wait_ge(o_taken[u], k)
                    for t in range(2):
                        cols = slice((2 * u + t) * P, (2 * u + t + 1) * P)
                        for d in range(KH):
                            mm(o_ps[u][:, t * D:(t + 1) * D], hi[j][d][:, cols], wT[:, d, :], start=(d == 0), stop=False)
                            last = mm(o_ps[u][:, t * D:(t + 1) * D], lo[j][d][:, cols], wT[:, d, :],
                                      start=False, stop=(d == KH - 1))
                    last.then_inc(o_mm[u], 1)

            pe.wait_ge(ident_loaded, 16)
            transposes(0, 0)
            pe.wait_ge(zeroed, 1)
            pe.wait_ge(wabs_done, 1)
            mm(y_ps[1][:, 0:1], ones[:, :], wabs[:, :], start=True, stop=True).then_inc(wsum_mm, 1)
            pe.wait_ge(mw_loaded, 16 * 3)
            for h in range(KH):
                last = mm(y_ps[0][:, h * C_ALL:(h + 1) * C_ALL], mw[:, h * P:(h + 1) * P], tapsum[:, :], start=True, stop=True)
            last.then_inc(taps_mm, 1)
            pe.wait_ge(W1l_done, 1)
            pe.wait_ge(W1h_done, 1)

            def first_phase(k, j, more=True):
                project(k, j)
                if more:
                    transposes(k + 1, 1 - j)
                feed_forward(k, j)

            project(0, 0)
            transposes(1, 1)
            pe.wait_ge(tern_done, 1)
            for d in range(KH):
                for o in range(KH):
                    last = nc.tensor.transpose(y_ps[1][:, d * D + o * P:d * D + (o + 1) * P], tern[:, o, d * P:(d + 1) * P], ident[:, :])
            last.then_inc(wT_mm, 1)
            pe.wait_ge(wT_done, 1)
            feed_forward(0, 0)
            first_phase(1, 1)
            with pe.Fori(1, CHUNKS // 2 - 1) as i:
                for j in range(2):
                    first_phase(2 * i + j, j)
            first_phase(CHUNKS - 2, 0)
            first_phase(CHUNKS - 1, 1, more=False)

            pe.wait_ge(xsum_done, 1)
            for h in range(KH):
                for d in range(KH):
                    last = mm(xT_ps[0][:, B * h:B * h + B], W1[:, d, h * P:(h + 1) * P], xsum[:, d, :],
                              start=(d == 0), stop=(d == KH - 1))
            last.then_inc(total_mm, 1)

            def filter_slot(i, s):
                pe.wait_ge(T_built[s], Q * (i + 1))
                pe.wait_ge(y_done[s % 2], i * (SLOTS // 2) + s // 2)
                for g in range(GS):
                    for lag in range(LAGS):
                        moving = p[:, ds(i * (SLOTS * GS) + s * GS + g, 1), :, LEAD - lag:LEAD - lag + NB]
                        last = mm(y_ps[s % 2][:, g * B * NB:(g + 1) * B * NB], T[s][:, g, lag, :, :].rearrange("p q j -> p (q j)"),
                                  moving.rearrange("p g b n -> p (g b) n"), start=(lag == 0), stop=(lag == LAGS - 1))
                last.then_inc(y_mm[s % 2], 1)

            for h in range(KH):
                pe.wait_ge(p_done[h], CHUNKS)
            pe.wait_ge(zeroed, 3 + SLOTS)
            filter_slot(0, 0)
            pe.wait_ge(W2_loaded, 16)
            pe.wait_ge(constT_done, 1)
            pe.wait_ge(tail_done, 1)
            for b in range(B):
                for h in range(KH):
                    last = mm(xT_ps[1][:, b * D:(b + 1) * D], constT[:, h, b, :], W2[:, h, :], start=(h == 0), stop=(h == KH - 1))
            last.then_inc(rows_mm, 1)
            for h in range(KH):
                last = mm(pT_ps[0][0:TAPS, 0:D], tail[:, h, :], W2[:, h, :], start=(h == 0), stop=(h == KH - 1))
            last.then_inc(edge_mm, 1)
            for s in range(1, SLOTS):
                filter_slot(0, s)
            with pe.Fori(1, USES) as i:
                for s in range(SLOTS):
                    filter_slot(i, s)

            pe.wait_ge(W2l_done, 1)
            for u in range(2):
                pe.wait_ge(o_taken[u], CHUNKS)
            pe.wait_ge(rows_done, 1)

            def output(k, j, reused=True):
                for h in range(KH):
                    pe.wait_ge(yhi_done[h], k + 1)
                    pe.wait_ge(ylo_done[h], k + 1)
                    for u in range(2):
                        if h == 0 and reused:
                            pe.wait_ge(out_done[u], k - 1)
                        for t in range(2):
                            cols = slice((2 * u + t) * P, (2 * u + t + 1) * P)
                            dst = out_ps[j][u][:, t * D:(t + 1) * D]
                            mm(dst, hi[j][h][:, cols], W2h[:, h, :], start=(h == 0 and t == 0), stop=False,
                               skip_group_check=True)
                            mm(dst, hi[j][h][:, cols], W2l[:, h, :], start=False, stop=False, skip_group_check=True)
                            last = mm(dst, lo[j][h][:, cols], W2h[:, h, :], start=False, stop=(h == KH - 1),
                                      skip_group_check=True)
                        if h == KH - 1:
                            last.then_inc(o_mm[u], 1)

            for j in range(2):
                output(j, j, False)
            with pe.Fori(1, CHUNKS // 2) as i:
                for j in range(2):
                    output(2 * i + j, j)


_INS = ["L0_attn_input_data", "L0_attn_W1", "L0_attn_bias1", "L0_attn_W2", "L0_attn_bias2",
        "L0_attn_memory_weights", "L0_ffn_weight", "L0_ffn_alpha", "L0_ffn_bias"]


def _constants(taps):
    import numpy as np
    m = np.zeros((taps + 2, 2 * taps + 3), np.float32)
    for d in range(taps):
        m[1 + d, d] = 1
        m[0, d] = -1
        m[1 + d, taps:taps + d] = -1
        m[0, taps + d] = taps - 1 - d
    m[1:taps + 1, 2 * taps] = 1
    m[0, 2 * taps] = -taps
    m[0, 2 * taps + 1] = 1
    m[taps + 1, 2 * taps + 2] = 1
    return {"ident": np.eye(128, dtype=np.float32), "tapsum": m}


def kernel(**inputs):
    import numpy as np
    import concourse.bacc as bacc
    from concourse.bass_utils import run_bass_kernel_spmd

    nc = bacc.Bacc("TRN2", target_bir_lowering=False, num_devices=1)
    arrays, args = {}, []
    consts = _constants(inputs["L0_attn_memory_weights"].shape[0] - 1)
    for name, a in [(n, inputs[n]) for n in _INS] + list(consts.items()):
        a = np.ascontiguousarray(a)
        arrays[f"in_{name}_dram"] = a
        args.append(nc.dram_tensor(f"in_{name}_dram", a.shape, mybir.dt.from_np(a.dtype), kind="ExternalInput").ap())
    shape = inputs["L0_attn_input_data"].shape
    args.append(nc.dram_tensor("out_dram", shape, mybir.dt.float32, kind="ExternalOutput").ap())
    fsmn_ternary_layer(nc, *args)
    r = run_bass_kernel_spmd(nc, [arrays], core_ids=[0])
    return r.results[0]["out_dram"]
```

```python
import concourse.bass as bass
from concourse import mybir
from contextlib import ExitStack



def fsmn_ternary_layer(nc, x_in, W1_in, b1_in, W2_in, b2_in, mw_in, w_in, alpha_in, bias_in,
                       ident_in, tapsum_in, out):
    f32 = mybir.dt.float32
    f32r = mybir.dt.float32r
    ALU = mybir.AluOpType
    ACT = mybir.ActivationFunctionType
    AX = mybir.AxisListType

    B, S, D = x_in.shape
    TAPS = mw_in.shape[0] - 1
    P = 128
    KH = D // P
    TILES = B * S // P
    CH = 4
    N = CH * P
    CHUNKS = TILES // CH
    CPB = CHUNKS // B
    L = 32
    Q = P // L
    NB = S // L
    LAGS = 2
    LATE = TAPS - 1 - L
    LEAD = LAGS - 1
    G = KH * L
    GS = 4
    DVE_Q = 3
    SLOTS = 4
    USES = G // GS // SLOTS
    RUN = LAGS * L
    WROW = RUN + L
    assert 0 <= LATE < L
    C_TAPS, C_TAIL, C_SUM, C_MW0, C_B1, C_ALL = 0, TAPS, 2 * TAPS, 2 * TAPS + 1, 2 * TAPS + 2, 2 * TAPS + 3
    EPS = 1e-5
    WARM = 16
    FIRST = 3
    THRESH = 0.7 / (D * D)

    x_dram = x_in.rearrange("b (t p) c -> p (b t) c", p=P)
    out_dram = out.rearrange("b (t p) c -> p (b t) c", p=P)
    taps_dram = nc.dram_tensor("padded_taps", [Q, G, WROW], f32, kind="Internal")

    ctx = ExitStack()
    with ctx:
        def sb(name, shape, dt=f32):
            return ctx.enter_context(nc.sbuf_tensor(name, shape, dt))

        def sem(name):
            return ctx.enter_context(nc.semaphore(name))

        x = sb("x", [P, TILES, D])
        p = sb("p", [P, G, B, LEAD + NB])
        runs = sb("runs", [P, G, RUN])
        T = [sb(f"T{s}", [P, GS, LAGS, Q, L]) for s in range(SLOTS)]
        ends = sb("ends", [P, KH, B * NB, LATE])
        late = sb("late", [P, KH, B * NB, LATE])
        y = sb("y", [P, G, B * NB])
        yT = [p[:, h * L:(h + 1) * L, :, :].rearrange("p g b n -> p (g b n)")[:, 0:B * S] for h in range(KH)]
        xn = [sb(f"xn{j}", [P, CH, D]) for j in range(2)]
        hi = [[sb(f"hi{j}{h}", [P, N], f32r) for h in range(KH)] for j in range(2)]
        lo = [[sb(f"lo{j}{h}", [P, N], f32r) for h in range(KH)] for j in range(2)]
        ffn = [sb(f"ffn{u}", [P, 2 * D]) for u in range(2)]
        stats = [sb(f"stats{j}", [P, CH, 6]) for j in range(2)]
        meanvar = [sb(f"meanvar{j}", [P, CH, 2]) for j in range(2)]
        eps = sb("eps", [P, 1])
        std = [sb(f"std{j}", [P, CH]) for j in range(2)]
        rinv = [sb(f"rinv{j}", [P, CH]) for j in range(2)]
        newt = [sb(f"newt{j}", [P, CH]) for j in range(2)]
        newt2 = [sb(f"newt2{j}", [P, CH]) for j in range(2)]
        rstd = [sb(f"rstd{j}", [P, CH]) for j in range(2)]
        shift = [sb(f"shift{j}", [P, CH]) for j in range(2)]
        ident = sb("ident", [P, P])
        ones = sb("ones", [P, P])
        tapsum = sb("tapsum", [TAPS + 2, C_ALL])
        mw = sb("mw", [TAPS + 2, D])
        W1 = sb("W1", [P, KH, D])
        W2 = sb("W2", [P, KH, D])
        W1h, W1l = sb("W1h", [P, KH, D], f32r), sb("W1l", [P, KH, D], f32r)
        W2h, W2l = sb("W2h", [P, KH, D], f32r), sb("W2l", [P, KH, D], f32r)
        w, tern = (ffn[u][:, :].rearrange("p (h d) -> p h d", h=KH) for u in range(2))
        wneg = y[:, 0:KH * D // (B * NB), :].rearrange("p (h e) n -> p h (e n)", h=KH)
        wabs = sb("wabs", [P, 1])
        warm = sb("warm", [P, 1])
        wT = sb("wT", [P, KH, D], f32r)
        delta = sb("delta", [P, 2])
        alpha = sb("alpha", [P, 1])
        biases = sb("biases", [P, 2, D])
        taps = sb("taps", [P, KH, C_ALL])
        wpad = sb("wpad", [P, KH, WROW])
        xsums = sb("xsums", [P, KH, CHUNKS])
        xsum = sb("xsum", [P, KH, B])
        total = sb("total", [P, KH, B])
        b1sum = sb("b1sum", [P, KH])
        const = sb("const", [P, KH, B])
        tail = sb("tail", [P, KH, TAPS])
        biasrow = sb("biasrow", [P, D])

        def bank(name):
            return ctx.enter_context(nc.psum_tensor(name, [P, N], f32))

        xT_ps = [bank(f"xT_ps{h}") for h in range(KH)]
        pT_ps = [bank(f"pT_ps{h}") for h in range(KH)]
        o_ps = [bank(f"o_ps{u}") for u in range(2)]
        y_ps = [bank(f"y_ps{u}") for u in range(2)]
        out_ps = [xT_ps, o_ps]
        last_ps = y_ps[0][:, 0:D]

        x_loaded = [sem(f"x_loaded{k}") for k in range(CHUNKS)]
        x0_loaded = [sem(f"x0_loaded{u}") for u in range(2)]
        W1_loaded, ident_loaded, mw_loaded = sem("W1_loaded"), sem("ident_loaded"), sem("mw_loaded")
        w_loaded, W2_loaded, small_loaded = sem("w_loaded"), sem("W2_loaded"), sem("small_loaded")
        zeroed = sem("zeroed")
        taps_mm, taps_done, wpad_done, taps_stored = sem("taps_mm"), sem("taps_done"), sem("wpad_done"), sem("taps_stored")
        wabs_done, wsum_mm, delta_done = sem("wabs_done"), sem("wsum_mm"), sem("delta_done")
        wneg_done, tern_done, wT_mm, wT_done = sem("wneg_done"), sem("tern_done"), sem("wT_mm"), sem("wT_done")
        W1h_done, W1l_done, W2h_done, W2l_done = sem("W1h_done"), sem("W1l_done"), sem("W2h_done"), sem("W2l_done")
        runs_loaded = sem("runs_loaded")
        T_built = [sem(f"T_built{s}") for s in range(SLOTS)]
        stats_done, agg_done, std_done = sem("stats_done"), sem("agg_done"), sem("std_done")
        rinv_done, newt_done, newt2_done, rstd_done = sem("rinv_done"), sem("newt_done"), sem("newt2_done"), sem("rstd_done")
        shift_done, xn_done = sem("shift_done"), sem("xn_done")
        xn_first = [sem(f"xn_first{e}") for e in range(2)]
        xT_mm = [sem(f"xT_mm{h}") for h in range(KH)]
        hi_done = [sem(f"hi_done{h}") for h in range(KH)]
        lo_done = [sem(f"lo_done{h}") for h in range(KH)]
        pT_mm = [sem(f"pT_mm{h}") for h in range(KH)]
        p_done = [sem(f"p_done{h}") for h in range(KH)]
        o_mm = [sem(f"o_mm{u}") for u in range(2)]
        o_taken = [sem(f"o_taken{u}") for u in range(2)]
        ffn_added = [sem(f"ffn_added{u}") for u in range(2)]
        xsum_done, total_mm, const_a, const_done = sem("xsum_done"), sem("total_mm"), sem("const_a"), sem("const_done")
        tail_done, biasrow_done, biases_added = sem("tail_done"), sem("biasrow_done"), sem("biases_added")
        edge_turned, yT0_done = sem("edge_turned"), sem("yT0_done")
        y_mm = [sem(f"y_mm{u}") for u in range(2)]
        y_done = [sem(f"y_done{u}") for u in range(2)]
        first_half_used = sem("first_half_used")
        ends_done = [sem(f"ends_done{h}") for h in range(KH)]
        late_done = sem("late_done")
        turned = [sem(f"turned{h}") for h in range(KH)]
        yT_done = [sem(f"yT_done{h}") for h in range(KH)]
        yhi_done = [sem(f"yhi_done{h}") for h in range(KH)]
        ylo_done = [sem(f"ylo_done{h}") for h in range(KH)]
        out_done = [sem(f"out_done{u}") for u in range(2)]
        out_stored = sem("out_stored")

        ds = bass.ds
        chunk_tiles = lambda k, first=0, count=CH: ds(k * CH + first, count)
        turn = lambda k: k + 2
        block = ctx.enter_context(nc.Block())

        def build_T(copy, s, q, use):
            rows_q = slice(q * L, (q + 1) * L)
            copy(T[s][rows_q, :, :, q, :],
                 runs[rows_q, ds(use * (SLOTS * GS) + s * GS, GS), :].rearrange("p g (l j) -> p g l j", j=L)
                 ).then_inc(T_built[s], 1)

        def add_late(engine, h, k, skip=0):
            first = yT[h][:, ds(k * N, N)].rearrange("p (n i) -> p n i", i=L)[:, skip:, 0:LATE]
            engine.tensor_tensor(first, first, late[:, h, ds(k * (N // L) + skip, N // L - skip), :],
                                 ALU.add).then_inc(yT_done[h], 1)

        @block.sync
        def _(sp):
            def load_x(k):
                sp.dma_start(x[:, k * CH:(k + 1) * CH, :], x_dram[:, k * CH:(k + 1) * CH, :]).then_inc(x_loaded[k], 16)

            for u in range(2):
                sp.dma_start(x[:, 2 * u:2 * u + 2, :], x_dram[:, 2 * u:2 * u + 2, :]).then_inc(x0_loaded[u], 16)
            sp.dma_start(W1[:, :, :], W1_in.rearrange("(h p) c -> p h c", p=P)).then_inc(W1_loaded, 16)
            sp.dma_start(ident[:, :], ident_in).then_inc(ident_loaded, 16)
            load_x(1)
            sp.dma_start(w, w_in.rearrange("(h p) d -> p h d", p=P)).then_inc(w_loaded, 16)
            sp.dma_start(mw[0:TAPS + 1, :], mw_in).then_inc(mw_loaded, 16)
            sp.dma_start(mw[TAPS + 1:TAPS + 2, :], b1_in.rearrange("(a c) -> a c", a=1)).then_inc(mw_loaded, 16)
            sp.dma_start(tapsum[:, :], tapsum_in).then_inc(mw_loaded, 16)
            load_x(2)
            sp.dma_start(alpha[:, :], alpha_in.partition_broadcast(P)).then_inc(small_loaded, 16)
            sp.dma_start(biases[:, 0, :], b2_in.partition_broadcast(P)).then_inc(small_loaded, 16)
            sp.dma_start(biases[:, 1, :], bias_in.partition_broadcast(P)).then_inc(small_loaded, 16)
            for k in range(3, CHUNKS // 2):
                load_x(k)
            sp.wait_ge(wpad_done, 1)
            for q in range(Q):
                sp.dma_start(taps_dram[q, :, :].rearrange("(h r) x -> r h x", h=KH),
                             wpad[q * L:(q + 1) * L, :, :]).then_inc(taps_stored, 16)
            for k in range(CHUNKS // 2, CHUNKS):
                load_x(k)
            sp.wait_ge(taps_stored, 16 * Q)
            for q in range(Q):
                sp.dma_start(runs[q * L:(q + 1) * L, :, :],
                             bass.AP(tensor=taps_dram, offset=q * G * WROW, ap=[[1, L], [WROW, G], [1, RUN]])
                             ).then_inc(runs_loaded, 16)
            sp.dma_start(W2[:, :, :], W2_in.rearrange("(h p) c -> p h c", p=P)).then_inc(W2_loaded, 16)

            def store(k, u):
                sp.wait_ge(out_done[u], k + 1)
                sp.dma_start(out_dram[:, chunk_tiles(k, 2 * u, 2), :], x[:, chunk_tiles(k, 2 * u, 2), :]
                             ).then_inc(out_stored, 16)

            with sp.Fori(0, CHUNKS - 1) as k:
                for u in range(2):
                    store(k, u)
            store(CHUNKS - 1, 0)
            for t in range(2):
                sp.wait_ge(out_done[1], CHUNKS + t)
                sp.dma_start(out_dram[:, TILES - 2 + t, :], x[:, TILES - 2 + t, :]).then_inc(out_stored, 16)
            sp.wait_ge(out_stored, 16 * (2 * CHUNKS + 1))

        @block.gpsimd
        def _(pool):
            nc.gpsimd.memset(ones[:, :], 1.0).then_inc(zeroed, 1)
            nc.gpsimd.memset(eps[:, :], EPS).then_inc(zeroed, 1)
            nc.gpsimd.memset(wpad[:, :, :], 0.0).then_inc(zeroed, 1)
            nc.gpsimd.memset(p[:, :, :, 0:LEAD], 0.0).then_inc(zeroed, 1)
            for s in range(SLOTS):
                if s == SLOTS - 1:
                    pool.wait_ge(W1h_done, 1)
                    nc.gpsimd.tensor_tensor(W1l[:, :, :], W1[:, :, :], W1h[:, :, :].bitcast(f32),
                                            ALU.subtract).then_inc(W1l_done, 1)
                nc.gpsimd.memset(T[s][:, :, :, :, :], 0.0).then_inc(zeroed, 1)
            pool.wait_ge(delta_done, 2)
            nc.gpsimd.tensor_scalar(wneg, w, delta[:, 1:2], None, ALU.is_lt).then_inc(wneg_done, 1)
            nc.gpsimd.tensor_scalar(tern, w, delta[:, 0:1], None, ALU.is_gt).then_inc(wneg_done, 1)
            pool.wait_ge(wneg_done, 2)
            nc.gpsimd.tensor_tensor(tern, tern, wneg, ALU.subtract).then_inc(tern_done, 1)
            pool.wait_ge(zeroed, 3)
            pool.wait_ge(taps_done, 1)
            nc.gpsimd.tensor_copy(wpad[:, :, L - 1:L - 1 + TAPS], taps[:, :, C_TAPS:C_TAPS + TAPS]).then_inc(wpad_done, 1)
            pool.wait_ge(small_loaded, 16 * 3)
            nc.gpsimd.tensor_tensor(biasrow[:, :], biases[:, 0, :], biases[:, 1, :], ALU.add).then_inc(biasrow_done, 1)

            def add_ffn(k):
                for u in range(2):
                    pool.wait_ge(o_taken[u], k + 1)
                    at = x[:, chunk_tiles(k, 2 * u, 2), :]
                    nc.gpsimd.tensor_tensor(at, at, ffn[u][:, :].rearrange("p (t c) -> p t c", t=2),
                                            ALU.add).then_inc(ffn_added[u], 1)

            def add_biases(k):
                at = x[:, ds(k * 2, 2), :]
                nc.gpsimd.tensor_tensor(at, at, biasrow[:, :].unsqueeze(1).to_broadcast([P, 2, D]),
                                        ALU.add).then_inc(biases_added, 1)

            pool.wait_ge(biasrow_done, 1)
            with pool.Fori(0, CHUNKS - 1) as k:
                add_ffn(k)
            with pool.Fori(0, 2 * (CHUNKS - 1)) as k:
                pool.wait_ge(ffn_added[1], CHUNKS - 1)
                add_biases(k)
            add_ffn(CHUNKS - 1)
            for u in range(2):
                pool.wait_ge(ffn_added[u], CHUNKS)
                add_biases(2 * (CHUNKS - 1) + u)

            def y_low(k, j):
                pool.wait_ge(yhi_done[0], k + 1)
                nc.gpsimd.tensor_tensor(lo[j][0][:, :], yT[0][:, ds(k * N, N)], hi[j][0][:, :].bitcast(f32),
                                        ALU.subtract).then_inc(ylo_done[0], 1)

            for j in range(2):
                y_low(j, j)
            pool.wait_ge(yT_done[1], 2)
            with pool.Fori(1, CHUNKS // 2) as i:
                for j in range(2):
                    pool.wait_ge(turned[1], 2 * i + j + 1)
                    add_late(nc.gpsimd, 1, 2 * i + j)
                    y_low(2 * i + j, j)

        @block.scalar
        def _(act):
            def root(n, j, tiles=slice(0, CH)):
                act.wait_ge(agg_done, n)
                nc.scalar.activation(std[j][:, tiles], meanvar[j][:, tiles, 1], ACT.Sqrt, bias=eps[:, 0:1]).then_inc(std_done, 1)

            def normalise_tile(k, j, t):
                return nc.scalar.activation(xn[j][:, t, :], x[:, k * CH + t, :], ACT.Identity,
                                            bias=shift[j][:, t:t + 1], scale=rstd[j][:, t:t + 1])

            def normalise_first(k, j):
                act.wait_ge(shift_done, turn(k) if k else 1)
                if k >= 2:
                    act.wait_ge(xT_mm[KH - 1], k - 1)
                for t in range(2):
                    normalise_tile(k, j, t).then_inc(xn_first[0], 1)

            def normalise(k, j):
                act.wait_ge(shift_done, turn(k))
                act.wait_ge(xT_mm[KH - 1], k - 1)
                for t in range(CH):
                    last = normalise_tile(k, j, t)
                last.then_inc(xn_done, 1)

            def x_high_half(k, j, h):
                act.wait_ge(xT_mm[h], k + 1)
                nc.scalar.activation(hi[j][h][:, :], xT_ps[h][:, :], ACT.Copy,
                                     accum_out=xsums[:, h, ds(k, 1)]).then_inc(hi_done[h], 1)

            def take_ffn(k):
                for u in range(2):
                    act.wait_ge(o_mm[u], k + 1)
                    act.wait_ge(ffn_added[u], k)
                    nc.scalar.activation(ffn[u][:, :], o_ps[u][:, :], ACT.Copy,
                                         scale=alpha[:, 0:1]).then_inc(o_taken[u], 1)

            def take_ends_half(k, h):
                act.wait_ge(p_done[h], k + 1)
                nc.scalar.activation(ends[:, h, ds(k * (N // L), N // L), :],
                                     pT_ps[h][:, :].rearrange("p (n i) -> p n i", i=L)[:, :, L - LATE:L],
                                     ACT.Copy).then_inc(ends_done[h], 1)

            def take_ends(k):
                for h in range(KH):
                    take_ends_half(k, h)

            act.wait_ge(zeroed, 2)
            nc.scalar.activation(warm[:, :], ones[:, 0:1], ACT.Sqrt)
            root(1, 0, slice(0, 2))
            act.wait_ge(W1_loaded, 16)
            nc.scalar.activation(W1h[:, :, :], W1[:, :, :], ACT.Copy).then_inc(W1h_done, 1)
            root(2, 0, slice(2, CH))
            normalise_first(0, 0)
            act.wait_ge(w_loaded, 16)
            nc.scalar.activation(wneg, w, ACT.Abs, accum_out=wabs[:, 0:1]).then_inc(wabs_done, 1)
            for h in range(KH):
                x_high_half(0, 0, h)
            act.wait_ge(wsum_mm, 1)
            for c, factor in enumerate((THRESH, -THRESH)):
                nc.scalar.activation(delta[:, c:c + 1], y_ps[1][:, 0:1], ACT.Copy, scale=factor).then_inc(delta_done, 1)
            root(turn(1), 1)
            act.wait_ge(taps_mm, 1)
            nc.scalar.activation(taps[:, :, :], y_ps[0][:, 0:KH * C_ALL].rearrange("p (h c) -> p h c", h=KH),
                                 ACT.Copy).then_inc(taps_done, 1)
            normalise_first(1, 1)
            for h in range(KH):
                take_ends_half(0, h)
                x_high_half(1, 1, h)
            root(turn(2), 0)
            act.wait_ge(wT_mm, 1)
            nc.scalar.activation(wT[:, :, :], y_ps[1][:, :].rearrange("p (h o) -> p h o", h=KH),
                                 ACT.Copy).then_inc(wT_done, 1)
            normalise_first(2, 0)
            act.wait_ge(small_loaded, 16 * 3)
            take_ffn(0)

            def first_phase(k, j, more=2):
                if more >= 2:
                    root(turn(k + 2), j)
                if more >= 1:
                    act.wait_ge(o_mm[1], k)
                for h in range(KH):
                    take_ends_half(k, h)
                    if more >= 1:
                        x_high_half(k + 1, 1 - j, h)
                if more >= 2:
                    normalise(k + 2, j)
                take_ffn(k)

            first_phase(1, 1)
            with act.Fori(1, CHUNKS // 2 - 1) as i:
                for j in range(2):
                    first_phase(2 * i + j, j)
            first_phase(CHUNKS - 2, 0, more=1)
            take_ends(CHUNKS - 1)
            act.wait_ge(W2_loaded, 16)
            nc.scalar.activation(W2h[:, :, :], W2[:, :, :], ACT.Copy).then_inc(W2h_done, 1)

            def take_y(i, s):
                act.wait_ge(y_mm[s % 2], i * (SLOTS // 2) + s // 2 + 1)
                nc.scalar.activation(y[:, ds(i * (SLOTS * GS) + s * GS, GS), :],
                                     y_ps[s % 2][:, :].rearrange("p (g n) -> p g n", g=GS),
                                     ACT.Copy).then_inc(y_done[s % 2], 1)

            def y_high_first(k, j, b, reused=True):
                act.wait_ge(yT_done[0], k + 1)
                chunk = yT[0][:, ds(k * N, N)]
                nc.scalar.activation(chunk, chunk, ACT.Identity, bias=const[:, 0, b:b + 1]).then_inc(yT0_done, 1)
                act.wait_ge(yT0_done, k + 1)
                if reused:
                    act.wait_ge(first_half_used, k - 1)
                nc.scalar.activation(hi[j][0][:, :], chunk, ACT.Copy).then_inc(yhi_done[0], 1)

            def y_high_second(k, j, b):
                act.wait_ge(yT_done[1], k + 1)
                nc.scalar.activation(hi[j][1][:, :], yT[1][:, ds(k * N, N)], ACT.Identity,
                                     bias=const[:, 1, b:b + 1]).then_inc(yhi_done[1], 1)

            def build(i, s):
                for q in range(DVE_Q, Q):
                    build_T(nc.scalar.copy, s, q, i)

            for s in range(2, SLOTS):
                build(0, s)
            with act.Fori(0, USES - 1) as i:
                for s in range(SLOTS):
                    take_y(i, s)
                    build(i + 1, s)
            take_ffn(CHUNKS - 1)
            for s in range(SLOTS):
                if s in (1, 2):
                    act.wait_ge(o_mm[1], s - 2 + CHUNKS)
                    y_high_first(s - 1, s - 1, 0, reused=False)
                take_y(USES - 1, s)
            for j in range(2):
                y_high_second(j, j, 0)
            for k in range(2, CHUNKS):
                y_high_first(k, k % 2, k // CPB)
                act.wait_ge(o_mm[1], k + CHUNKS - 1)
                y_high_second(k, k % 2, k // CPB)

        @block.vector
        def _(dve):
            V = nc.vector

            def tile_statistics(k, j, tiles):
                for t in tiles:
                    V.bn_stats(stats[j][:, t, :], x[:, k * CH + t, :]).then_inc(stats_done, 1)

            def aggregate(k, j, tiles):
                dve.wait_ge(stats_done, k * CH + tiles[-1] + 1)
                for t in tiles:
                    last = V.bn_aggr(meanvar[j][:, t, :], stats[j][:, t, :])
                last.then_inc(agg_done, 1)

            def statistics(k, j):
                dve.wait_ge(x_loaded[k], 16)
                tile_statistics(k, j, range(CH))
                aggregate(k, j, range(CH))

            def invert(n, j, tiles=slice(0, CH)):
                dve.wait_ge(std_done, n)
                V.reciprocal(rinv[j][:, tiles], std[j][:, tiles]).then_inc(rinv_done, 1)

            def newton_a(n, j, tiles=slice(0, CH)):
                dve.wait_ge(rinv_done, n)
                V.scalar_tensor_tensor(newt[j][:, tiles], rinv[j][:, tiles], -0.5, rinv[j][:, tiles],
                                       ALU.mult, ALU.mult).then_inc(newt_done, 1)

            def newton_b(n, j, tiles=slice(0, CH)):
                dve.wait_ge(newt_done, n)
                V.scalar_tensor_tensor(newt2[j][:, tiles], meanvar[j][:, tiles, 1], EPS, newt[j][:, tiles],
                                       ALU.add, ALU.mult).then_inc(newt2_done, 1)

            def newton_c(n, j, tiles=slice(0, CH)):
                dve.wait_ge(newt2_done, n)
                V.scalar_tensor_tensor(rstd[j][:, tiles], newt2[j][:, tiles], 1.5, rinv[j][:, tiles],
                                       ALU.add, ALU.mult).then_inc(rstd_done, 1)

            def shifts(n, j, tiles=slice(0, CH)):
                dve.wait_ge(rstd_done, n)
                V.scalar_tensor_tensor(shift[j][:, tiles], meanvar[j][:, tiles, 0], -1.0, rstd[j][:, tiles],
                                       ALU.mult, ALU.mult).then_inc(shift_done, 1)

            def x_low(k, j, h):
                dve.wait_ge(hi_done[h], k + 1)
                V.tensor_tensor(lo[j][h][:, :], xT_ps[h][:, :], hi[j][h][:, :].bitcast(f32),
                                ALU.subtract).then_inc(lo_done[h], 1)

            def to_filter_layout(k, h):
                dve.wait_ge(pT_mm[h], k + 1)
                dst = p[:, h * L:(h + 1) * L, ds(k // CPB, 1), ds((k % CPB) * (N // L) + LEAD, N // L)]
                V.transpose(dst.rearrange("p r b n -> p (b n) r"),
                            pT_ps[h][:, :].rearrange("p (n i) -> p n i", i=L)[:, :, ::-1]).then_inc(p_done[h], 1)

            def normalise_rest(k, j):
                dve.wait_ge(shift_done, turn(k))
                if k >= 2:
                    dve.wait_ge(xT_mm[KH - 1], k - 1)
                for t in range(2, CH):
                    V.tensor_scalar(xn[j][:, t, :], x[:, k * CH + t, :], rstd[j][:, t:t + 1], shift[j][:, t:t + 1],
                                    ALU.mult, ALU.add).then_inc(xn_first[1], 1)

            a, b = slice(0, 2), slice(2, CH)
            dve.wait_ge(x0_loaded[0], 16)
            tile_statistics(0, 0, range(2))
            aggregate(0, 0, range(2))
            dve.wait_ge(x0_loaded[1], 16)
            tile_statistics(0, 0, range(2, CH))
            invert(1, 0, a)
            aggregate(0, 0, range(2, CH))
            newton_a(1, 0, a)
            newton_b(1, 0, a)
            newton_c(1, 0, a)
            shifts(1, 0, a)
            invert(2, 0, b)
            newton_a(2, 0, b)
            newton_b(2, 0, b)
            newton_c(2, 0, b)
            shifts(2, 0, b)
            normalise_rest(0, 0)

            def invert_fully(k, j):
                invert(turn(k), j)
                newton_a(turn(k), j)
                newton_b(turn(k), j)
                newton_c(turn(k), j)
                shifts(turn(k), j)

            statistics(1, 1)
            x_low(0, 0, 0)
            x_low(0, 0, 1)
            invert_fully(1, 1)
            normalise_rest(1, 1)
            to_filter_layout(0, 0)
            to_filter_layout(0, 1)
            dve.wait_ge(x_loaded[2], 16)
            tile_statistics(2, 0, range(2))
            x_low(1, 1, 0)
            x_low(1, 1, 1)
            tile_statistics(2, 0, range(2, CH))
            aggregate(2, 0, range(CH))
            invert_fully(2, 0)
            normalise_rest(2, 0)

            def first_phase(k, j, more=2):
                if more >= 2:
                    statistics(k + 2, j)
                to_filter_layout(k, 0)
                if more >= 2:
                    invert(turn(k + 2), j)
                to_filter_layout(k, 1)
                if more >= 2:
                    newton_a(turn(k + 2), j)
                    newton_b(turn(k + 2), j)
                    newton_c(turn(k + 2), j)
                    shifts(turn(k + 2), j)
                if more >= 1:
                    x_low(k + 1, 1 - j, 0)
                    x_low(k + 1, 1 - j, 1)

            for k in range(1, CHUNKS - 2):
                first_phase(k, k % 2)
            dve.wait_ge(runs_loaded, 16 * Q)
            dve.wait_ge(zeroed, 4 + SLOTS)

            def build_slot(s, i):
                for q in range(DVE_Q if i or s >= 2 else Q):
                    build_T(V.tensor_copy, s, q, i)

            build_slot(0, 0)
            first_phase(CHUNKS - 2, 0, more=1)
            build_slot(1, 0)
            V.tensor_reduce(xsum[:, :, :], xsums[:, :, :].rearrange("p h (b k) -> p h b k", b=B),
                            axis=AX.X, op=ALU.add).then_inc(xsum_done, 1)
            first_phase(CHUNKS - 1, 1, more=0)

            def add_late_tap(h, m):
                tap = taps[:, h, L + 1 + m:L + 2 + m]
                src = ends[:, h, 0:B * NB - 2, LATE - 1 - m:LATE]
                dst = late[:, h, 2:B * NB, 0:m + 1]
                if m == LATE - 1:
                    dve.wait_ge(ends_done[h], CHUNKS)
                    V.tensor_scalar(dst, src, tap, None, ALU.mult).then_inc(late_done, 1)
                else:
                    dve.wait_ge(late_done, h * LATE + LATE - 1 - m)
                    V.scalar_tensor_tensor(dst, src, tap, dst, ALU.mult, ALU.add).then_inc(late_done, 1)

            def add_edge(h, k):
                first = yT[h][:, k * N:k * N + TAPS]
                return V.tensor_tensor(first, first, tail[:, h, :], ALU.add)

            def from_filter_layout(h, k, edge=False):
                src = y[:, h * L:(h + 1) * L, ds(k * (N // L), N // L)].rearrange("p r n -> p n r")
                last = V.transpose(yT[h][:, ds(k * N, N)].rearrange("p (n i) -> p n i", i=L), src)
                if edge:
                    last.then_inc(edge_turned, 1)
                    dve.wait_ge(edge_turned, 1)
                    last = add_edge(h, k)
                last.then_inc(turned[h], 1)

            def add_late_here(h, k):
                dve.wait_ge(turned[h], k + 1)
                if k % CPB == 0:
                    add_edge(h, k)
                    add_late(V, h, k, skip=2)
                else:
                    add_late(V, h, k)

            def rebuild_slot(i, s):
                dve.wait_ge(y_mm[s % 2], (i - 1) * (SLOTS // 2) + s // 2 + 1)
                build_slot(s, i)

            for s in range(2, SLOTS):
                build_slot(s, 0)
            dve.wait_ge(taps_done, 1)
            V.tensor_tensor(b1sum[:, :], taps[:, :, C_B1], taps[:, :, C_SUM], ALU.mult).then_inc(const_a, 1)
            for h in range(KH):
                last = V.tensor_scalar(tail[:, h, :], taps[:, h, C_TAIL:C_TAIL + TAPS], taps[:, h, C_B1:C_B1 + 1], None, ALU.mult)
            last.then_inc(tail_done, 1)
            dve.wait_ge(total_mm, 1)
            for h in range(KH):
                V.scalar_tensor_tensor(total[:, h, :], taps[:, h, C_B1:C_B1 + 1].to_broadcast([P, B]), float(S),
                                       xT_ps[0][:, B * h:B * h + B], ALU.mult, ALU.add).then_inc(const_a, 1)
            dve.wait_ge(const_a, 1 + KH)
            for h in range(KH):
                V.tensor_scalar(const[:, h, :], total[:, h, :], taps[:, h, C_MW0:C_MW0 + 1], b1sum[:, h:h + 1],
                                ALU.mult, ALU.add).then_inc(const_done, 1)
            late_taps = [(h, m) for h in range(KH) for m in reversed(range(LATE))]
            for i in range(1, USES - 1):
                for s in range(SLOTS):
                    rebuild_slot(i, s)
                    for h, m in late_taps[:2]:
                        add_late_tap(h, m)
                    late_taps = late_taps[2:]
            dve.wait_ge(W2h_done, 1)
            V.tensor_tensor(W2l[:, :, :], W2[:, :, :], W2h[:, :, :].bitcast(f32), ALU.subtract).then_inc(W2l_done, 1)
            for u in range(2):
                dve.wait_ge(y_done[u], G // GS // KH // 2)
            dve.wait_ge(late_done, KH * LATE)
            for b in range(1, B):
                V.memset(late[:, :, b * NB:b * NB + 2, :], 0.0).then_inc(late_done, 1)
            dve.wait_ge(late_done, KH * LATE + B - 1)
            dve.wait_ge(tail_done, 1)
            for s in range(SLOTS):
                rebuild_slot(USES - 1, s)
                chunks = range(s * CHUNKS // SLOTS, (s + 1) * CHUNKS // SLOTS)
                for k in chunks:
                    from_filter_layout(0, k)
                for k in chunks:
                    add_late_here(0, k)
            for u in range(2):
                dve.wait_ge(y_done[u], G // GS // 2)

            def y_low(k, j):
                dve.wait_ge(yhi_done[1], k + 1)
                V.scalar_tensor_tensor(lo[j][1][:, :], yT[1][:, ds(k * N, N)], const[:, 1, k // CPB:k // CPB + 1],
                                       hi[j][1][:, :].bitcast(f32), ALU.add, ALU.subtract).then_inc(ylo_done[1], 1)

            def finish(k, u):
                dve.wait_ge(o_mm[u], k + CHUNKS + 1)
                at = x[:, chunk_tiles(k, 2 * u, 2), :]
                V.tensor_tensor(at, out_ps[k % 2][u][:, :].rearrange("p (t c) -> p t c", t=2), at,
                                ALU.add).then_inc(out_done[u], 1)

            dve.wait_ge(const_done, KH)
            from_filter_layout(1, 0)
            add_late_here(1, 0)
            from_filter_layout(1, 1)
            add_late_here(1, 1)
            y_low(0, 0)
            from_filter_layout(1, 2)
            y_low(1, 1)
            dve.wait_ge(biases_added, 2 * CHUNKS)
            for k in range(CHUNKS - 1):
                finish(k, 0)
                if 1 <= k < CHUNKS - 3:
                    from_filter_layout(1, k + 3, edge=((k + 3) % CPB == 0))
                finish(k, 1)
                if k + 2 < CHUNKS:
                    y_low(k + 2, k % 2)
                if k == 0:
                    from_filter_layout(1, 3)
            finish(CHUNKS - 1, 0)
            for t in range(2):
                dve.wait_ge(o_mm[1], 2 * CHUNKS + t)
                at = x[:, TILES - 2 + t, :]
                V.tensor_tensor(at, last_ps[:, :] if t else out_ps[(CHUNKS - 1) % 2][1][:, 0:D], at,
                                ALU.add).then_inc(out_done[1], 1)

        @block.tensor
        def _(pe):
            mm = nc.tensor.matmul

            def transposes(k, j):
                pe.wait_ge(xn_done, k - FIRST + 1)
                for h in range(KH):
                    pe.wait_ge(lo_done[h], k)
                    for t in range(CH):
                        last = nc.tensor.transpose(xT_ps[h][:, t * P:(t + 1) * P], xn[j][:, t, h * P:(h + 1) * P], ident[:, :])
                    last.then_inc(xT_mm[h], 1)

            def project(k, j):
                project_high(k, j)
                project_low(k, j)

            def project_high(k, j):
                for d in range(KH):
                    pe.wait_ge(hi_done[d], k + 1)
                    for h in range(KH):
                        if d == 0:
                            pe.wait_ge(ends_done[h], k)
                        mm(pT_ps[h][:, :], W1h[:, d, h * P:(h + 1) * P], hi[j][d][:, :], start=(d == 0), stop=False)
                        mm(pT_ps[h][:, :], W1l[:, d, h * P:(h + 1) * P], hi[j][d][:, :], start=False, stop=False)

            def project_low(k, j):
                for h in range(KH):
                    for d in range(KH):
                        if h == 0:
                            pe.wait_ge(lo_done[d], k + 1)
                        last = mm(pT_ps[h][:, :], W1h[:, d, h * P:(h + 1) * P], lo[j][d][:, :],
                                  start=False, stop=(d == KH - 1))
                    last.then_inc(pT_mm[h], 1)

            def feed_forward(k, j, pairs=range(2)):
                for u in pairs:
                    pe.wait_ge(o_taken[u], k)
                    for t in range(2):
                        cols = slice((2 * u + t) * P, (2 * u + t + 1) * P)
                        for d in range(KH):
                            mm(o_ps[u][:, t * D:(t + 1) * D], hi[j][d][:, cols], wT[:, d, :], start=(d == 0), stop=False)
                            last = mm(o_ps[u][:, t * D:(t + 1) * D], lo[j][d][:, cols], wT[:, d, :],
                                      start=False, stop=(d == KH - 1))
                    last.then_inc(o_mm[u], 1)

            pe.wait_ge(zeroed, 1)
            for _ in range(WARM):
                mm(y_ps[1][:, 0:P], ones[:, :], ones[:, :], start=True, stop=True)
            pe.wait_ge(ident_loaded, 16)

            def first_transposes(k, j):
                for t in (0, 2, 1, 3):
                    pe.wait_ge(xn_first[t // 2], 2 * k + t % 2 + 1)
                    for h in range(KH):
                        if t == 0 and k > 0:
                            pe.wait_ge(lo_done[h], k)
                        last = nc.tensor.transpose(xT_ps[h][:, t * P:(t + 1) * P], xn[j][:, t, h * P:(h + 1) * P], ident[:, :])
                        if t == CH - 1:
                            last.then_inc(xT_mm[h], 1)

            first_transposes(0, 0)
            pe.wait_ge(wabs_done, 1)
            mm(y_ps[1][:, 0:1], ones[:, :], wabs[:, :], start=True, stop=True).then_inc(wsum_mm, 1)
            pe.wait_ge(mw_loaded, 16 * 3)
            for h in range(KH):
                last = mm(y_ps[0][:, h * C_ALL:(h + 1) * C_ALL], mw[:, h * P:(h + 1) * P], tapsum[:, :], start=True, stop=True)
            last.then_inc(taps_mm, 1)
            pe.wait_ge(W1l_done, 1)
            pe.wait_ge(W1h_done, 1)

            def first_phase(k, j):
                project(k, j)
                transposes(k + 1, 1 - j)
                feed_forward(k, j)

            project(0, 0)
            first_transposes(1, 1)
            project_high(1, 1)
            pe.wait_ge(tern_done, 1)
            for d in range(KH):
                for o in range(KH):
                    last = nc.tensor.transpose(y_ps[1][:, d * D + o * P:d * D + (o + 1) * P], tern[:, o, d * P:(d + 1) * P], ident[:, :])
            last.then_inc(wT_mm, 1)
            project_low(1, 1)
            pe.wait_ge(wT_done, 1)
            feed_forward(0, 0)
            first_transposes(2, 0)
            feed_forward(1, 1)
            with pe.Fori(1, CHUNKS // 2 - 1) as i:
                for j in range(2):
                    first_phase(2 * i + j, j)
            project(CHUNKS - 2, 0)
            transposes(CHUNKS - 1, 1)
            feed_forward(CHUNKS - 2, 0, [0])
            project(CHUNKS - 1, 1)
            feed_forward(CHUNKS - 2, 0, [1])

            def filter_slot(i, s):
                pe.wait_ge(T_built[s], Q * (i + 1))
                pe.wait_ge(y_done[s % 2], i * (SLOTS // 2) + s // 2)
                for g in range(GS):
                    for lag in range(LAGS):
                        moving = p[:, ds(i * (SLOTS * GS) + s * GS + g, 1), :, LEAD - lag:LEAD - lag + NB]
                        last = mm(y_ps[s % 2][:, g * B * NB:(g + 1) * B * NB], T[s][:, g, lag, :, :].rearrange("p q j -> p (q j)"),
                                  moving.rearrange("p g b n -> p (g b) n"), start=(lag == 0), stop=(lag == LAGS - 1))
                last.then_inc(y_mm[s % 2], 1)

            pe.wait_ge(taps_done, 1)
            pe.wait_ge(p_done[0], CHUNKS)
            pe.wait_ge(zeroed, 4 + SLOTS)
            filter_slot(0, 0)
            pe.wait_ge(xsum_done, 1)
            for h in range(KH):
                for d in range(KH):
                    last = mm(xT_ps[0][:, B * h:B * h + B], W1[:, d, h * P:(h + 1) * P], xsum[:, d, :],
                              start=(d == 0), stop=(d == KH - 1))
            last.then_inc(total_mm, 1)
            for s in range(1, SLOTS):
                filter_slot(0, s)
            pe.wait_ge(p_done[1], CHUNKS)
            with pe.Fori(1, USES - 1) as i:
                for s in range(SLOTS):
                    filter_slot(i, s)
            feed_forward(CHUNKS - 1, 1)
            for s in range(SLOTS):
                filter_slot(USES - 1, s)

            pe.wait_ge(W2l_done, 1)
            pe.wait_ge(const_done, KH)

            def output_tiles(k, j, h, tiles, dst):
                cols = [slice(t * P, (t + 1) * P) for t in tiles]
                pe.wait_ge(yhi_done[h], k + 1)
                for c in range(len(tiles)):
                    mm(dst[c], hi[j][h][:, cols[c]], W2h[:, h, :], start=(h == 0 and c == 0), stop=False,
                       skip_group_check=True)
                    mm(dst[c], hi[j][h][:, cols[c]], W2l[:, h, :], start=False, stop=False, skip_group_check=True)
                pe.wait_ge(ylo_done[h], k + 1)
                for c in range(len(tiles)):
                    last = mm(dst[c], lo[j][h][:, cols[c]], W2h[:, h, :], start=False, stop=(h == KH - 1),
                              skip_group_check=True)
                return last

            def output_half(k, j, h, reused=True):
                for u in range(2):
                    if h == 0 and reused:
                        pe.wait_ge(out_done[u], k - 1)
                    last = output_tiles(k, j, h, range(2 * u, 2 * u + 2),
                                        [out_ps[j][u][:, t * D:(t + 1) * D] for t in range(2)])
                    if h == KH - 1:
                        last.then_inc(o_mm[u], 1)
                if h == 0:
                    last.then_inc(first_half_used, 1)

            output_half(0, 0, 0, reused=False)
            for u in range(2):
                pe.wait_ge(o_taken[u], CHUNKS)
            output_half(1, 1, 0, reused=False)
            for j in range(2):
                output_half(j, j, 1)
            with pe.Fori(1, CHUNKS // 2 - 1) as i:
                for j in range(2):
                    for h in range(KH):
                        output_half(2 * i + j, j, h)
            for h in range(KH):
                output_half(CHUNKS - 2, 0, h)
            o_last, chunk = out_ps[1], CHUNKS - 1
            for u in range(2):
                pe.wait_ge(out_done[u], chunk - 1)
            for tiles, dst, u in ((range(0, 2), [o_last[0][:, 0:D], o_last[0][:, D:2 * D]], 0),
                                  ([2], [o_last[1][:, 0:D]], 1),
                                  ([3], [last_ps], 1)):
                for h in range(KH):
                    last = output_tiles(chunk, 1, h, tiles, dst)
                last.then_inc(o_mm[u], 1)


_INS = ["L0_attn_input_data", "L0_attn_W1", "L0_attn_bias1", "L0_attn_W2", "L0_attn_bias2",
        "L0_attn_memory_weights", "L0_ffn_weight", "L0_ffn_alpha", "L0_ffn_bias"]


def _constants(taps):
    import numpy as np
    m = np.zeros((taps + 2, 2 * taps + 3), np.float32)
    for d in range(taps):
        m[1 + d, d] = 1
        m[0, d] = -1
        m[1 + d, taps:taps + d] = -1
        m[0, taps + d] = taps - 1 - d
    m[1:taps + 1, 2 * taps] = 1
    m[0, 2 * taps] = -taps
    m[0, 2 * taps + 1] = 1
    m[taps + 1, 2 * taps + 2] = 1
    return {"ident": np.eye(128, dtype=np.float32), "tapsum": m}


def kernel(**inputs):
    import numpy as np
    import concourse.bacc as bacc
    from concourse.bass_utils import run_bass_kernel_spmd

    nc = bacc.Bacc("TRN2", target_bir_lowering=False, num_devices=1)
    arrays, args = {}, []
    consts = _constants(inputs["L0_attn_memory_weights"].shape[0] - 1)
    for name, a in [(n, inputs[n]) for n in _INS] + list(consts.items()):
        a = np.ascontiguousarray(a)
        arrays[f"in_{name}_dram"] = a
        args.append(nc.dram_tensor(f"in_{name}_dram", a.shape, mybir.dt.from_np(a.dtype), kind="ExternalInput").ap())
    shape = inputs["L0_attn_input_data"].shape
    args.append(nc.dram_tensor("out_dram", shape, mybir.dt.float32, kind="ExternalOutput").ap())
    fsmn_ternary_layer(nc, *args)
    r = run_bass_kernel_spmd(nc, [arrays], core_ids=[0])
    return r.results[0]["out_dram"]
```
